# Optimizing a Trainium2 kernel written in Bass

```python
import numpy as np
import jax
import jax.numpy as jnp

def _softmax(x, axis=-1):
    return jax.nn.softmax(x, axis=axis)

def _gelu(x):
    return jax.nn.gelu(x, approximate=True)

def _silu(x):
    return jax.nn.silu(x)

def _sigmoid(x):
    return jax.nn.sigmoid(x)

def _layernorm(x, axis=-1, eps=1e-05):
    m = jnp.mean(x, axis=axis, keepdims=True)
    v = jnp.var(x, axis=axis, keepdims=True)
    return (x - m) / jnp.sqrt(v + eps)

def _scatter_add(tgt, idx, src, axis=0):
    return tgt.at[idx].add(src)

def _segment_sum(src, seg, n):
    return jax.ops.segment_sum(src, seg, n)
kernel_name = 'mk_sandwich_d1_jaxref_r4_75e187'

def setup_inputs(seed: int=0):
    np.random.seed(seed)
    _w = jnp.asarray

    def _L0_attn_setup():
        import jax, jax.numpy as jnp
        import numpy as np
        EMBED = 1024
        HEADS = 16
        HEAD_DIM = EMBED // HEADS
        ROT = 64
        B, S = (1, 512)
        MASK_VAL = -1000000000.0

        def _rotate_every_two(x):
            r = jnp.stack((x[..., 1::2], x[..., ::2]), axis=-1)
            return r.reshape(x.shape)

        def _fixed_pos_embedding(seq_len, rot_dim):
            inv_freq = 1.0 / 10000.0 ** (jnp.arange(0, rot_dim, 2, dtype=jnp.float32) / rot_dim)
            t = jnp.arange(seq_len, dtype=jnp.float32)
            sinusoid = jnp.einsum('i,j->ij', t, inv_freq)
            return (jnp.sin(sinusoid), jnp.cos(sinusoid))

        def _apply_rotary(x, sin, cos):
            sin = jnp.repeat(sin[None, :, None, :], 2, axis=3)
            cos = jnp.repeat(cos[None, :, None, :], 2, axis=3)
            return x * cos + _rotate_every_two(x) * sin
        key = jax.random.key(seed)
        ks = jax.random.split(key, 5)
        sc = 0.02
        return {'hidden_states': jax.random.normal(ks[0], (B, S, EMBED), jnp.float32), 'Wq': jax.random.normal(ks[1], (EMBED, EMBED), jnp.float32) * sc, 'Wk': jax.random.normal(ks[2], (EMBED, EMBED), jnp.float32) * sc, 'Wv': jax.random.normal(ks[3], (EMBED, EMBED), jnp.float32) * sc, 'Wo': jax.random.normal(ks[4], (EMBED, EMBED), jnp.float32) * sc}
    _L0_attn_in = _L0_attn_setup()

    def _L0_ffn_setup():
        import jax, jax.numpy as jnp
        import numpy as np
        LORA_RANK = 16
        LORA_ALPHA = 16
        LORA_SCALE = LORA_ALPHA / LORA_RANK
        key = jax.random.key(seed)
        k1, k2, k3, k4, k5 = jax.random.split(key, 5)
        B, S, D_IN, D_OUT, N_LORA, R = (8, 512, 1024, 1024, 3, LORA_RANK)
        std = 1.0 / np.sqrt(D_IN)
        x = jax.random.normal(k1, (B, S, D_IN), dtype=jnp.float32)
        weight = jax.random.truncated_normal(k2, -3.0, 3.0, (D_OUT, D_IN), dtype=jnp.float32) * std
        bias = jax.random.normal(k3, (D_OUT,), dtype=jnp.float32) * 0.01
        lora_A = jax.random.normal(k4, (N_LORA, R, D_IN), dtype=jnp.float32) * std
        lora_B = jax.random.normal(k5, (N_LORA, D_OUT, R), dtype=jnp.float32) * 0.02
        lora_start_indices = jnp.arange(4, dtype=jnp.int64) * 2
        return {'x': x, 'weight': weight, 'bias': bias, 'lora_A': lora_A, 'lora_B': lora_B, 'lora_start_indices': lora_start_indices}
    _L0_ffn_in = _L0_ffn_setup()
    _d = {'L0_attn_hidden_states': _L0_attn_in['hidden_states'], 'L0_attn_Wq': _L0_attn_in['Wq'], 'L0_attn_Wk': _L0_attn_in['Wk'], 'L0_attn_Wv': _L0_attn_in['Wv'], 'L0_attn_Wo': _L0_attn_in['Wo'], 'L0_ffn_weight': _L0_ffn_in['weight'], 'L0_ffn_bias': _L0_ffn_in['bias'], 'L0_ffn_lora_A': _L0_ffn_in['lora_A'], 'L0_ffn_lora_B': _L0_ffn_in['lora_B'], 'L0_ffn_lora_start_indices': _L0_ffn_in['lora_start_indices']}
    _x0 = _d['L0_attn_hidden_states']
    _d['L0_attn_hidden_states'] = jax.random.normal(jax.random.fold_in(jax.random.key(seed), 1), (8, 512, 1024), dtype=_x0.dtype)
    del _x0
    return _d

def reference(L0_attn_hidden_states, L0_attn_Wq, L0_attn_Wk, L0_attn_Wv, L0_attn_Wo, L0_ffn_weight, L0_ffn_bias, L0_ffn_lora_A, L0_ffn_lora_B, L0_ffn_lora_start_indices):

    def _L0_attn_ref(hidden_states, Wq, Wk, Wv, Wo):
        import jax, jax.numpy as jnp
        import numpy as np
        EMBED = 1024
        HEADS = 16
        HEAD_DIM = EMBED // HEADS
        ROT = 64
        B, S = (1, 512)
        MASK_VAL = -1000000000.0

        def _rotate_every_two(x):
            r = jnp.stack((x[..., 1::2], x[..., ::2]), axis=-1)
            return r.reshape(x.shape)

        def _fixed_pos_embedding(seq_len, rot_dim):
            inv_freq = 1.0 / 10000.0 ** (jnp.arange(0, rot_dim, 2, dtype=jnp.float32) / rot_dim)
            t = jnp.arange(seq_len, dtype=jnp.float32)
            sinusoid = jnp.einsum('i,j->ij', t, inv_freq)
            return (jnp.sin(sinusoid), jnp.cos(sinusoid))

        def _apply_rotary(x, sin, cos):
            sin = jnp.repeat(sin[None, :, None, :], 2, axis=3)
            cos = jnp.repeat(cos[None, :, None, :], 2, axis=3)
            return x * cos + _rotate_every_two(x) * sin
        b, s, e = hidden_states.shape
        q = (hidden_states @ Wq).reshape(b, s, HEADS, HEAD_DIM)
        k = (hidden_states @ Wk).reshape(b, s, HEADS, HEAD_DIM)
        v = (hidden_states @ Wv).reshape(b, s, HEADS, HEAD_DIM)
        sin, cos = _fixed_pos_embedding(s, ROT)
        q = jnp.concatenate([_apply_rotary(q[..., :ROT], sin, cos), q[..., ROT:]], axis=-1)
        k = jnp.concatenate([_apply_rotary(k[..., :ROT], sin, cos), k[..., ROT:]], axis=-1)
        q = q.transpose(0, 2, 1, 3)
        k = k.transpose(0, 2, 1, 3)
        v = v.transpose(0, 2, 1, 3)
        logits = jnp.einsum('bhqd,bhkd->bhqk', q, k)
        causal = jnp.tril(jnp.ones((s, s), dtype=bool))[None, None]
        logits = jnp.where(causal, logits, MASK_VAL)
        logits = logits / jnp.sqrt(jnp.float32(HEAD_DIM))
        attn = jax.nn.softmax(logits, axis=-1)
        out = jnp.einsum('bhqk,bhkd->bhqd', attn, v)
        out = out.transpose(0, 2, 1, 3).reshape(b, s, e)
        return out @ Wo

    def _L0_ffn_ref(x, weight, bias, lora_A, lora_B, lora_start_indices):
        import jax, jax.numpy as jnp
        import numpy as np
        LORA_RANK = 16
        LORA_ALPHA = 16
        LORA_SCALE = LORA_ALPHA / LORA_RANK
        y = jnp.einsum('bsd,od->bso', x, weight) + bias
        B = x.shape[0]
        seg = jnp.searchsorted(lora_start_indices, jnp.arange(B), side='right') - 1
        adapter_idx = jnp.clip(seg - 1, 0, lora_A.shape[0] - 1)
        A = lora_A[adapter_idx]
        Bw = lora_B[adapter_idx]
        lo = jnp.einsum('bsr,bor->bso', jnp.einsum('bsd,brd->bsr', x, A), Bw) * LORA_SCALE
        use_lora = (seg > 0)[:, None, None]
        return y + jnp.where(use_lora, lo, jnp.zeros((), dtype=y.dtype))
    x = L0_attn_hidden_states
    x = x + _layernorm(_L0_attn_ref(_layernorm(x, axis=-1), L0_attn_Wq, L0_attn_Wk, L0_attn_Wv, L0_attn_Wo), axis=-1)
    x = x + _layernorm(_L0_ffn_ref(_layernorm(x, axis=-1), L0_ffn_weight, L0_ffn_bias, L0_ffn_lora_A, L0_ffn_lora_B, L0_ffn_lora_start_indices), axis=-1)
    return x

_drawn_inputs = setup_inputs


def setup_inputs(seed=0):
    import zlib

    import numpy as np

    out = dict(_drawn_inputs(seed))
    spreads = {}
    factors = {'L0_ffn_bias': 8.0}
    for name, (base, spread) in spreads.items():
        noise = np.random.default_rng([zlib.crc32(name.encode()), seed]).standard_normal(out[name].shape)
        drawn = base * np.exp(spread * noise) if base else spread * noise
        out[name] = jnp.asarray(drawn.astype(out[name].dtype))
    for name, factor in factors.items():
        out[name] = (out[name] * factor).astype(out[name].dtype)
    return out
```

```python
from contextlib import ExitStack

import concourse.bass as bass
from concourse import mybir

ALU = mybir.AluOpType
ACT = mybir.ActivationFunctionType
AX = mybir.AxisListType
F32 = mybir.dt.float32
F16 = mybir.dt.float16
I32 = mybir.dt.int32
ABSMAX = bass.bass_isa.ReduceOp.absmax

PART = 128
B, S, D = 8, 512, 1024
HEADS, HD = 16, 64
KT = D // PART
ST = S // PART
PAIRS = HEADS // 2
TILES = B * ST
NLORA, RANK, NSEG = 3, 16, 4
LR = NLORA * RANK
LOW_ROW = 64
CHUNKS, KC = 4, KT // 4

EPS = 1e-5
XS = 2.0 ** 10
XS2 = XS ** -2
V_DOWN = 2.0 ** -20
QK_DOWN = 2.0 ** -21
T_DOWN = 2.0 ** -20
ONE = 2.0 ** 14
P_LOG = 9.704060527839234
NEG = -1e30
LOWEST = -3e38

Q_ORDER = (3, 2, 0, 1)
S_OFF = {3: 0, 2: 512, 0: 896, 1: 1024}
S_LEN = 1280
BLOCKS = [(j, kt) for j in Q_ORDER for kt in range(j + 1)]
PT_GROUPS = ((0, 4), (4, 8), (8, 10))

BANK_Q, BANK_K, BANK_S, BANK_PT, BANK_O = 0, 1, 2, 5, 7
BANK_FF, BANK_AO, BANK_T, BANK_TR = 0, 2, 4, 5

C_ID = 0
C_MASK = C_ID + 128
C_COS = C_MASK + 512
C_SIN = C_COS + 512
C_BIASROW = C_SIN + 512
C_TB = C_BIASROW + 1
C_CODE = C_TB + TILES
C_HALF = C_CODE + 1
C_LEN = C_HALF + 4

W_V, W_Q, W_K, W_O, W_F = range(5)


def sandwich_kernel(nc, x, wq, wk, wv, wo, wf, bias, lora_a, lora_b, starts, consts, out):
    x_v = x.rearrange("b (t p) d -> b t p d", p=PART)
    x_tiles = x.rearrange("b (t p) d -> (b t) p d", p=PART)
    out_tiles = out.rearrange("b (t p) d -> (b t) p d", p=PART)
    raw_dram = [w.rearrange("(k p) n -> p k n", p=PART) for w in (wv, wq, wk, wo, wf)]
    a_dram = lora_a.rearrange("(k p) r -> p k r", p=PART)
    attn = nc.dram_tensor("attn_scratch", (B * S, D), F32, kind="Internal").ap()
    attn_pairs = attn.rearrange("(b t p) (h c) -> b h p t c", b=B, p=PART, h=PAIRS)
    attn_tiles = attn.rearrange("(i p) d -> i p d", p=PART)

    with ExitStack() as ctx:
        def sb(name, shape, dt):
            return ctx.enter_context(nc.sbuf_tensor(name, shape, dt))

        def sem(name):
            return ctx.enter_context(nc.semaphore(name))

        region = [sb(f"region{i}", [PART, KT, 2, D], F16) for i in range(3)]
        w_dst = {W_V: region[2], W_Q: region[0], W_K: region[1], W_O: region[2], W_F: region[0]}
        arena1 = sb("arena1", [PART, 9216], F32)
        arena2 = sb("arena2", [PART, 8192], F32)
        raw1 = arena1[:, 0:8192].rearrange("p (k n) -> p k n", k=KT)
        raw2 = arena2[:, :].rearrange("p (k n) -> p k n", k=KT)
        raw_r1 = region[1][:, :, :, :].rearrange("p k h n -> p (k h n)").bitcast(F32).rearrange(
            "p (k n) -> p k n", k=KT)
        w_raw = {W_V: raw1, W_Q: raw_r1, W_K: raw1, W_O: raw2, W_F: raw2}

        x_ring = arena2[:, 0:4096].rearrange("p (t d) -> p t d", t=ST)

        def half(ap, shape):
            return ap.bitcast(F16).rearrange(shape[0], **shape[1])

        xnt_shape = ("p (k h t) -> p k h t", dict(k=KT, h=2))
        xnt = [half(arena2[:, 4096:8192], xnt_shape), half(arena1[:, 0:4096], xnt_shape)]
        scores = arena1[:, 4096:4096 + 2 * S_LEN].rearrange("p (a n) -> p a n", a=2)
        pt = half(arena1[:, 6656:6656 + S_LEN], ("p (h n q) -> p h n q", dict(h=2, q=PART)))
        o_pair = arena1[:, 7936:7936 + 1024].rearrange("p (a t c) -> p a t c", a=2, t=ST)

        v_split = sb("v_split", [PART, ST, HEADS, 2 * HD], F16)
        q_stack = sb("q_stack", [PART, 2, 2, S], F16)
        k_stack = sb("k_stack", [PART, 2, 2, S], F16)
        k_low = sb("k_low", [PART, 2, S], F16)
        swapped = sb("swapped", [PART, S], F32)
        rotated = sb("rotated", [PART, S], F32)
        o_low = sb("o_low", [PART, ST, HD], F32)
        o_sum_t = sb("o_sum_t", [PART, ST, HD], F32)
        con = sb("con", [PART, C_LEN], F32)
        ident = con[:, C_ID:C_ID + 128]
        causal = con[:, C_MASK:C_MASK + 512]
        cos_t = con[:, C_COS:C_COS + 512]
        sin_t = con[:, C_SIN:C_SIN + 512]
        row_max = sb("row_max", [PART, 2, ST], F32)
        exp_bias = sb("exp_bias", [PART, 2, ST], F32)
        row_sum = sb("row_sum", [PART, 2, ST], F32)
        row_inv = sb("row_inv", [PART, 2, ST], F32)
        bn = sb("bn", [PART, ST, 2, 6], F32)
        mean_var = sb("mean_var", [PART, ST, 2], F32)
        var_s = sb("var_s", [PART, ST], F32)
        rstd = sb("rstd", [PART, ST], F32)
        w_part = sb("w_part", [PART, 5, CHUNKS], F32)
        w_pmax = sb("w_pmax", [PART, 8], F32)
        w_max = sb("w_max", [PART, 8], F32)
        expo_i = sb("expo_i", [PART, 8], I32)
        expo = sb("expo", [PART, 12], F32)
        field = sb("field", [PART, 2], F32)
        field_i = sb("field_i", [PART, 1], I32)
        pow2 = sb("pow2", [PART, 16], F32)
        S_SM, S_NEG, S_KAPPA, S_A, S_B, S_BIAS, S_KF, S_ROWS, S_NOTBIAS = range(5, 14)
        starts_i = sb("starts_i", [LR, NSEG], I32)
        starts_f = sb("starts_f", [LR, NSEG], F32)
        le = sb("le", [LR, NSEG, TILES], F32)
        adapter = sb("adapter", [LR, TILES], F32)

        r1f = region[1][:, :, :, :].rearrange("p k h n -> p (k h n)").bitcast(F32)
        o_in = r1f[:, 0:2048].rearrange("p (a d) -> p a d", a=2)
        x2 = r1f[:, 2048:4096].rearrange("p (a d) -> p a d", a=2)
        y_out = r1f[:, 4096:6144].rearrange("p (a d) -> p a d", a=2)
        o_t = half(r1f[:, 6144:7168], ("p (k h t) -> p k h t", dict(k=KT, h=2)))
        xn2_t = half(r1f[:, 7168:8192], ("p (k h t) -> p k h t", dict(k=KT, h=2)))
        u1 = arena1[:, 0:1024]
        u2 = arena1[:, 1024:2048]
        xn2 = arena1[:, 2048:3072]
        b_raw = arena1[:, 3072:4096]
        b_split = half(arena1[:, 4096:5120], ("p (h n) -> p h n", dict(h=2)))
        a_raw = arena1[:, 5120:5120 + KT * LR].rearrange("p (k r) -> p k r", k=KT)
        a_split = half(arena1[:, 5504:5504 + KT * LR], ("p (k h r) -> p k h r", dict(k=KT, h=2)))
        t_f = arena1[0:LR, 5888:6016]
        t_stack = arena1[:, 6016:6080].bitcast(F16)

        ps = ctx.enter_context(nc.psum_tensor("ps", [PART, 8, 512], F32))
        ps_o = ps[:, BANK_O, :].rearrange("p (t c) -> p t c", t=ST)

        const_in = sem("const_in")
        raw_in = [[sem(f"raw_in_{w}_{c}") for c in range(CHUNKS)] for w in range(5)]
        x_in = [sem(f"x_in{t}") for t in range(ST)]
        lora_in = sem("lora_in")
        o_stored = [sem(f"o_stored{a}") for a in range(2)]
        part_max_done = sem("part_max_done")
        pmax_done = sem("pmax_done")
        max_done = sem("max_done")
        scale_done = sem("scale_done")
        w_high_done = sem("w_high_done")
        w_low_done = sem("w_low_done")
        dve_step = sem("dve_step")
        bn_done = sem("bn_done")
        meanvar_done = sem("meanvar_done")
        var_done = sem("var_done")
        rstd_done = sem("rstd_done")
        xn_done = sem("xn_done")
        xt_done = sem("xt_done")
        xt_high = sem("xt_high")
        xt_low = sem("xt_low")
        qk_done = sem("qk_done")
        qk_drained = sem("qk_drained")
        rot_mul = sem("rot_mul")
        rot_done = sem("rot_done")
        qk_high = sem("qk_high")
        qk_low = sem("qk_low")
        v_done = sem("v_done")
        v_high = sem("v_high")
        v_low = sem("v_low")
        s_done = sem("s_done")
        masked = sem("masked")
        bias_done = sem("bias_done")
        exp_done = sem("exp_done")
        pt_done = sem("pt_done")
        pt_high = sem("pt_high")
        pt_low = sem("pt_low")
        pv_done = sem("pv_done")
        o_copied = sem("o_copied")
        o_added = sem("o_added")
        inv_done = sem("inv_done")
        o_ready = sem("o_ready")
        o_tile_in = [sem(f"o_tile_in{a}") for a in range(2)]
        x_tile_in = [sem(f"x_tile_in{a}") for a in range(2)]
        y_stored = [sem(f"y_stored{a}") for a in range(2)]
        ot_done = sem("ot_done")
        ot_high = sem("ot_high")
        ot_low = sem("ot_low")
        ao_done = sem("ao_done")
        bn1_done = sem("bn1_done")
        mv1_done = sem("mv1_done")
        var1_done = sem("var1_done")
        pow1_done = sem("pow1_done")
        rm1_done = sem("rm1_done")
        u1_done = sem("u1_done")
        x2_done = sem("x2_done")
        bnx_done = sem("bnx_done")
        mvx_done = sem("mvx_done")
        varx_done = sem("varx_done")
        powx_done = sem("powx_done")
        xn2_done = sem("xn2_done")
        x2t_done = sem("x2t_done")
        x2t_high = sem("x2t_high")
        x2t_low = sem("x2t_low")
        lt_done = sem("lt_done")
        lt_scaled = sem("lt_scaled")
        lt_high = sem("lt_high")
        lt_low = sem("lt_low")
        lora_ready = sem("lora_ready")
        ff_done = sem("ff_done")
        bn2_done = sem("bn2_done")
        mv2_done = sem("mv2_done")
        var2_done = sem("var2_done")
        pow2_done = sem("pow2_done")
        rm2_done = sem("rm2_done")
        u2_done = sem("u2_done")
        y_done = sem("y_done")

        mv1 = sb("mv1", [PART, 2], F32)
        st1 = sb("st1", [PART, 2, 6], F32)
        sm1 = sb("sm1", [PART, 4], F32)
        mvx = sb("mvx", [PART, 2], F32)
        stx = sb("stx", [PART, 2, 6], F32)
        smx = sb("smx", [PART, 2], F32)
        mv2 = sb("mv2", [PART, 2], F32)
        st2 = sb("st2", [PART, 2, 6], F32)
        sm2 = sb("sm2", [PART, 4], F32)

        def need(eng, semaphore, count):
            if isinstance(count, int) and count <= 0:
                return
            eng.wait_ge(semaphore, count)

        def over_batches(eng, body):
            body(0, 0)
            with eng.Fori(0, (B - 2) // 2) as it:
                body(2 * it + 1, 1)
                body(2 * it + 2, 2)
            body(B - 1, B - 1)

        def over_tiles(eng, body):
            for i in range(4):
                body(i, i, i // 2)
            with eng.Fori(0, (TILES - 6) // 2) as it:
                body(2 * it + 4, 4, it + 2)
                body(2 * it + 5, 5, it + 2)
            for i in range(TILES - 2, TILES + 2):
                body(i, i, i // 2)

        block = ctx.enter_context(nc.Block())

        @block.sync
        def _(sp):
            sp.dma_start(con[:, :], consts).then_inc(const_in, 16)
            sp.dma_start(starts_i[:, :], starts).then_inc(const_in, 16)

            def load_raw(w, c):
                sp.dma_start(w_raw[w][:, KC * c:KC * (c + 1), :],
                             raw_dram[w][:, KC * c:KC * (c + 1), :]).then_inc(raw_in[w][c], 16)

            for t in range(ST):
                sp.dma_start(x_ring[:, t, :], x_v[0, t]).then_inc(x_in[t], 16)
            for w in (W_V, W_Q):
                for c in range(CHUNKS):
                    load_raw(w, c)
            for c in range(CHUNKS):
                sp.wait_ge(w_low_done, CHUNKS * W_V + c + 1)
                load_raw(W_K, c)

            def batch(b, kind):
                if kind < B - 1:
                    for t in range(ST):
                        sp.wait_ge(xt_done, 8 * b + 2 * t + 2)
                        sp.dma_start(x_ring[:, t, :], x_v[b + 1, t]).then_inc(x_in[t], 16)
                else:
                    sp.wait_ge(xt_done, 8 * B)
                    sp.wait_ge(qk_done, 2 * PAIRS * (B - 1))
                    sp.wait_ge(v_done, 8 * (B - 1))
                    for c in range(CHUNKS):
                        load_raw(W_O, c)
                if kind > 0:
                    sp.wait_ge(o_ready, 16 * b)
                    sp.dma_start(attn_pairs[b - 1, PAIRS - 1], o_pair[:, 1]).then_inc(o_stored[1], 16)
                for p in range(PAIRS - 1):
                    if kind == B - 1 and p == 5:
                        for c in range(CHUNKS):
                            sp.wait_ge(w_low_done, CHUNKS * W_O + c + 1)
                            load_raw(W_F, c)
                    sp.wait_ge(o_ready, 16 * b + 2 * p + 2)
                    sp.dma_start(attn_pairs[b, p], o_pair[:, p % 2]).then_inc(o_stored[p % 2], 16)

            over_batches(sp, batch)

            sp.wait_ge(o_ready, HEADS * B)
            sp.dma_start(attn_pairs[B - 1, PAIRS - 1], o_pair[:, 1]).then_inc(o_stored[1], 16)
            for a in range(2):
                sp.wait_ge(o_stored[a], 16 * PAIRS * B // 2)
            sp.wait_ge(lora_ready, 1)
            sp.dma_start(a_raw, a_dram).then_inc(lora_in, 16)
            sp.dma_start(b_raw[0:LR, :], lora_b).then_inc(lora_in, 16)
            sp.dma_start(b_raw[LOW_ROW:LOW_ROW + LR, :], lora_b).then_inc(lora_in, 16)
            sp.dma_start(b_raw[LR:LR + 1, :], bias).then_inc(lora_in, 16)

            def load_tile(i, a):
                sp.dma_start(o_in[:, a], attn_tiles[i]).then_inc(o_tile_in[a], 16)

            load_tile(0, 0)
            load_tile(1, 1)

            def step(i, kind, i2):
                a = kind % 2
                if kind >= 2:
                    if kind < TILES:
                        sp.wait_ge(y_done, i - 1)
                if kind < TILES:
                    sp.dma_start(x2[:, a], x_tiles[i]).then_inc(x_tile_in[a], 16)
                if kind <= TILES - 3:
                    sp.wait_ge(ot_done, 2 * i + 2)
                    load_tile(i + 2, a)
                if kind >= 2:
                    sp.wait_ge(y_done, i - 1)
                    sp.dma_start(out_tiles[i - 2], y_out[:, a]).then_inc(y_stored[a], 16)

            over_tiles(sp, step)
            for a in range(2):
                sp.wait_ge(y_stored[a], 16 * TILES // 2)

        @block.tensor
        def _(pe):
            mm = nc.tensor.matmul

            def x_transposes(ring_t, hh, b_count):
                need(pe, xt_low, b_count)
                for k in range(4):
                    last = nc.tensor.transpose(ps[:, BANK_K, 128 * k:128 * k + 128],
                                               x_ring[:, ring_t, 512 * hh + 128 * k:512 * hh + 128 * k + 128],
                                               ident)
                last.then_inc(xt_done, 1)

            def qk_product(which, pair, par, ks):
                w, bank = region[which], (BANK_Q, BANK_K)[which]
                cols = slice(128 * pair, 128 * pair + 128)
                for k in ks:
                    o = ps[:, bank, :]
                    mm(o, w[:, k, 0, cols], xnt[par][:, k, 0, :], start=(k == 0), stop=False)
                    mm(o, w[:, k, 0, cols], xnt[par][:, k, 1, :], start=False, stop=False)
                    last = mm(o, w[:, k, 1, cols], xnt[par][:, k, 0, :], start=False, stop=(k == KT - 1))
                if ks[-1] == KT - 1:
                    last.then_inc(qk_done, 1)

            def v_product(t, h8, par, ks):
                cols = slice(512 * h8, 512 * h8 + 512)
                tok = slice(128 * t, 128 * t + 128)
                for k in ks:
                    o = ps[:, BANK_Q, :]
                    mm(o, xnt[par][:, k, 0, tok], region[2][:, k, 0, cols], start=(k == 0), stop=False)
                    mm(o, xnt[par][:, k, 0, tok], region[2][:, k, 1, cols], start=False, stop=False)
                    last = mm(o, xnt[par][:, k, 1, tok], region[2][:, k, 0, cols], start=False, stop=(k == KT - 1))
                if ks[-1] == KT - 1:
                    last.then_inc(v_done, 1)

            def pt_group(g, a):
                first, end = PT_GROUPS[g]
                for n in range(first, end):
                    j, kt = BLOCKS[n]
                    last = nc.tensor.transpose(ps[:, BANK_PT + g % 2, 128 * (n - first):128 * (n - first) + 128],
                                               scores[:, a, S_OFF[j] + 128 * kt:S_OFF[j] + 128 * kt + 128], ident)
                last.then_inc(pt_done, 1)

            def score_products(a, par):
                hrow = slice(64 * a, 64 * a + 64)
                for j in Q_ORDER:
                    n = 128 * (j + 1)
                    qs = slice(128 * j, 128 * j + 128)
                    flat = ps[:, BANK_S:BANK_S + 3, :].rearrange("p b n -> p (b n)")
                    o = flat[:, S_OFF[j]:S_OFF[j] + n]
                    mm(o, q_stack[:, par, a, qs], k_stack[:, par, a, 0:n], start=True, stop=False)
                    last = mm(o, q_stack[hrow, par, a, qs], k_low[hrow, par, 0:n], start=False, stop=True)
                    if j != 2:
                        last.then_inc(s_done, 1)

            def pv_products(head):
                for n, (j, kt) in enumerate(BLOCKS):
                    mm(ps_o[:, j, :], pt[:, 0, n, :], v_split[:, kt, head, :], start=(kt == 0), stop=False)
                    last = mm(ps_o[:, j, 0:HD], pt[:, 1, n, :], v_split[:, kt, head, 0:HD], start=False,
                              stop=(kt == j))
                last.then_inc(pv_done, 1)

            pe.wait_ge(const_in, 32)
            for t in range(ST):
                pe.wait_ge(xn_done, t + 1)
                for hh in range(2):
                    x_transposes(t, hh, 2 * t + hh)
            pe.wait_ge(xt_low, 8)
            for t in range(ST):
                if t == 0:
                    for c in range(CHUNKS):
                        pe.wait_ge(w_low_done, CHUNKS * W_V + c + 1)
                        v_product(0, 0, 0, range(KC * c, KC * (c + 1)))
                else:
                    pe.wait_ge(v_low, t)
                    v_product(t, 0, 0, range(KT))
            pe.wait_ge(v_low, ST)
            for which, w in ((0, W_Q), (1, W_K)):
                for c in range(CHUNKS):
                    pe.wait_ge(w_low_done, CHUNKS * w + c + 1)
                    qk_product(which, 0, 0, range(KC * c, KC * (c + 1)))

            def head_slot(b, kind, p, a):
                first, last_b = kind == 0, kind == B - 1
                bp = kind % 2
                g = 16 * b + 2 * p + a
                pr = 8 * b + p
                prev = not (first and p == 0 and a == 0)
                has_qk = not (last_b and p == PAIRS - 1)
                has_v = not (last_b and p >= 4)
                has_xt = not last_b and p < 4
                if prev:
                    need(pe, exp_done, 4 * g)
                    need(pe, pt_low, 3 * g - 3)
                    pt_group(0, 1 - a)
                    pt_group(1, 1 - a)
                if a == 0:
                    need(pe, qk_low, 2 * pr + 2)
                    need(pe, qk_high, 2 * pr + 2)
                need(pe, masked, 4 * g)
                score_products(a, p % 2)

                def late_transposes():
                    if prev:
                        need(pe, pt_low, 3 * g - 2)
                        pt_group(2, 1 - a)

                def pv():
                    if prev:
                        head = (2 * p + a - 1) % HEADS
                        need(pe, pt_high, 3 * g)
                        need(pe, pt_low, 3 * g)
                        if 0 < 2 * p + a:
                            need(pe, v_low, 8 * b + (4 if head < 8 else 8))
                        need(pe, o_added, g - 1)
                        pv_products(head)

                n_pair, n_par = (p + 1) % PAIRS, (p + 1) % 2
                n_bp = bp if p < PAIRS - 1 else 1 - bp
                v_bp = bp if p < 4 else 1 - bp
                if a == 0:
                    if has_qk:
                        need(pe, v_low, 4 + pr if not (last_b and p > 4) else 8 * B)
                        need(pe, qk_drained, 2 * pr + 2)
                        if p == PAIRS - 1:
                            need(pe, xt_low, 8 * b + 16)
                        qk_product(0, n_pair, n_bp, [0, 1, 2])
                    late_transposes()
                    if has_qk:
                        qk_product(0, n_pair, n_bp, [3, 4, 5, 6, 7])
                    pv()
                    if has_qk:
                        need(pe, xt_low, 8 * B if last_b else 8 * b + 8 + 2 * min(p, 4))
                        qk_product(1, n_pair, n_bp, range(KT))
                else:
                    if has_v:
                        need(pe, qk_drained, 2 * pr + 3)
                        if p == 4:
                            need(pe, xt_low, 8 * b + 16)
                        v_product(p % 4, 1 if p < 4 else 0, v_bp, [0, 1, 2])
                    late_transposes()
                    if has_v:
                        v_product(p % 4, 1 if p < 4 else 0, v_bp, [3, 4, 5])
                    if has_xt:
                        need(pe, qk_drained, 2 * pr + 4)
                        need(pe, xn_done, 4 * b + 4 + p + 1)
                        x_transposes(p, 0, 8 * b + 8 + 2 * p)
                    pv()
                    if has_v:
                        v_product(p % 4, 1 if p < 4 else 0, v_bp, [6, 7])
                    if has_xt:
                        x_transposes(p, 1, 8 * b + 8 + 2 * p + 1)

            def batch(b, kind):
                for p in range(PAIRS):
                    for a in range(2):
                        head_slot(b, kind, p, a)

            over_batches(pe, batch)
            g = HEADS * B
            pe.wait_ge(exp_done, 4 * g)
            pe.wait_ge(pt_low, 3 * g - 3)
            pt_group(0, 1)
            pt_group(1, 1)
            pe.wait_ge(pt_low, 3 * g - 2)
            pt_group(2, 1)
            pe.wait_ge(pt_high, 3 * g)
            pe.wait_ge(pt_low, 3 * g)
            pe.wait_ge(o_added, g - 1)
            pv_products(HEADS - 1)

            def tile_transposes(src, done):
                for hh in range(2):
                    for k in range(4):
                        last = nc.tensor.transpose(ps[:, BANK_TR + hh, 128 * k:128 * k + 128],
                                                   src[:, 512 * hh + 128 * k:512 * hh + 128 * k + 128], ident)
                    last.then_inc(done, 1)

            def product(act_t, w, bank, last_one):
                for k in range(KT):
                    for hl, wl in ((0, 0), (0, 1), (1, 0)):
                        for c in range(2):
                            final = last_one and k == KT - 1 and hl == 1
                            last = mm(ps[:, bank + c, :], act_t[:, k, hl, :], w[:, k, wl, 512 * c:512 * c + 512],
                                      start=(k == 0 and hl == 0 and wl == 0), stop=final)
                return last

            def step(i, kind, i2):
                a = kind % 2
                if 1 <= kind <= TILES:
                    need(pe, xn2_done, i)
                    if kind < TILES:
                        need(pe, ot_low, 2 * i + 2)
                    tile_transposes(xn2, x2t_done)
                if kind < TILES:
                    if kind == 0:
                        pe.wait_ge(o_tile_in[0], 16)
                        pe.wait_ge(pt_low, 3 * g)
                        tile_transposes(o_in[:, 0], ot_done)
                        pe.wait_ge(w_low_done, CHUNKS * W_O + CHUNKS)
                    need(pe, ot_low, 2 * i + 2)
                    need(pe, ot_high, 2 * i + 2)
                    need(pe, u1_done, i)
                    product(o_t, region[2], BANK_AO, True).then_inc(ao_done, 1)
                if 1 <= kind <= TILES:
                    need(pe, x2t_low, 2 * i)
                    need(pe, x2t_high, 2 * i)
                    need(pe, lora_ready, 2)
                    need(pe, lt_scaled, i - 1)
                    for k in range(KT):
                        for ah, xh in ((0, 0), (0, 1), (1, 0)):
                            last = mm(ps[0:LR, BANK_T, 0:128], a_split[:, k, ah, :], xn2_t[:, k, xh, :],
                                      start=(k == 0 and ah == 0 and xh == 0), stop=(k == KT - 1 and ah == 1))
                    last.then_inc(lt_done, 1)
                if kind <= TILES - 2:
                    na = 1 - a
                    need(pe, o_tile_in[na], 16 * (i2 + 1 + a))
                    need(pe, x2t_low, 2 * i)
                    tile_transposes(o_in[:, na], ot_done)
                if 1 <= kind <= TILES:
                    if kind == 1:
                        pe.wait_ge(w_low_done, CHUNKS * W_F + CHUNKS)
                    need(pe, u2_done, i - 1)
                    product(xn2_t, region[0], BANK_FF, False)
                    need(pe, lt_low, i)
                    for c in range(2):
                        cols = slice(512 * c, 512 * c + 512)
                        mm(ps[:, BANK_FF + c, :], t_stack, b_split[:, 0, cols], start=False, stop=False)
                        last = mm(ps[:, BANK_FF + c, :], t_stack, b_split[:, 1, cols], start=False, stop=True)
                    last.then_inc(ff_done, 1)

            over_tiles(pe, step)

        @block.vector
        def _(dve):
            v = nc.vector
            steps = [0]

            def chained(ins):
                steps[0] += 1
                ins.then_inc(dve_step, 1)
                dve.wait_ge(dve_step, steps[0])

            def part_max(w, c):
                dve.wait_ge(raw_in[w][c], 16)
                v.tensor_reduce(w_part[:, w, c:c + 1], w_raw[w][:, KC * c:KC * (c + 1), :], AX.XY, ALU.max,
                                apply_absolute_value=True).then_inc(part_max_done, 1)

            def join_max(w):
                dve.wait_ge(part_max_done, CHUNKS * (w + 1))
                v.tensor_reduce(w_pmax[:, w:w + 1], w_part[:, w, :], AX.X, ALU.max).then_inc(pmax_done, 1)

            def exponents(first, n):
                cols = slice(first, first + n)
                chained(v.tensor_scalar(expo_i[:, cols], w_max[:, cols].bitcast(I32), 23, None,
                                        ALU.logical_shift_right))
                chained(v.tensor_scalar(expo[:, cols], expo_i[:, cols], 30.0, None, ALU.max))

            def power(col, src, sign, plus):
                chained(v.tensor_scalar(field[:, 0:1], src, float(sign), float(plus), ALU.mult, ALU.add))
                chained(v.tensor_scalar(field_i[:, 0:1], field[:, 0:1], 1.0, 254.0, ALU.max, ALU.min))
                chained(v.tensor_scalar(pow2[:, col:col + 1].bitcast(I32), field_i[:, 0:1], 23, None,
                                        ALU.logical_shift_left))

            def weight_scale(w):
                dve.wait_ge(max_done, w + 1)
                exponents(w, 1)
                power(w, expo[:, w:w + 1], -1, 268)
                v.tensor_copy(pow2[:, 15:16], pow2[:, w:w + 1]).then_inc(scale_done, 1)

            def split_low(w, c):
                dve.wait_ge(w_high_done, CHUNKS * w + c + 1)
                ks = slice(KC * c, KC * (c + 1))
                v.scalar_tensor_tensor(w_dst[w][:, ks, 1, :], w_raw[w][:, ks, :], pow2[:, w:w + 1],
                                       w_dst[w][:, ks, 0, :], ALU.mult, ALU.subtract).then_inc(w_low_done, 1)

            def ln_stats(t, n):
                for c in range(2):
                    v.bn_stats(bn[:, t, c, :], x_ring[:, t, 512 * c:512 * c + 512]).then_inc(bn_done, 1)
                need(dve, bn_done, 2 * n + 2)
                v.nop(nofuse=True)
                v.bn_aggr(mean_var[:, t, :], bn[:, t, :, :].rearrange("p a b -> p (a b)")).then_inc(meanvar_done, 1)
                need(dve, meanvar_done, n + 1)
                v.tensor_scalar(var_s[:, t:t + 1], mean_var[:, t, 1:2], EPS, XS2, ALU.add,
                                ALU.mult).then_inc(var_done, 1)

            def ln_apply(t, n):
                need(dve, rstd_done, n + 1)
                v.tensor_scalar(x_ring[:, t, :], x_ring[:, t, :], mean_var[:, t, 0:1], rstd[:, t:t + 1],
                                ALU.subtract, ALU.mult).then_inc(xn_done, 1)

            def xt_evac(t, hh, par, n):
                need(dve, xt_high, n + 1)
                dst = xnt[par][:, 4 * hh:4 * hh + 4, :, 128 * t:128 * t + 128]
                v.tensor_tensor(dst[:, :, 1, :], ps[:, BANK_K, :].rearrange("p (k t) -> p k t", k=4),
                                dst[:, :, 0, :], ALU.subtract).then_inc(xt_low, 1)

            def v_evac(t, h8, n):
                need(dve, v_high, n + 1)
                dst = v_split[:, t, 8 * h8:8 * h8 + 8, :]
                v.scalar_tensor_tensor(dst[:, :, HD:2 * HD], ps[:, BANK_Q, :].rearrange("p (h c) -> p h c", h=8),
                                       V_DOWN, dst[:, :, 0:HD], ALU.mult, ALU.subtract).then_inc(v_low, 1)

            def qk_drain(which, n):
                bank = (BANK_Q, BANK_K)[which]
                need(dve, qk_done, n + 1)
                need(dve, qk_high, n)
                need(dve, qk_low, n)
                v.tensor_tensor(rotated[:, :], ps[:, bank, :], cos_t, ALU.mult)
                v.stream_shuffle(swapped[:, :], ps[:, bank, :], [r ^ 1 for r in range(32)]).then_inc(qk_drained, 1)

            def qk_low_parts(which, par, n):
                need(dve, rot_done, n + 1)
                need(dve, qk_high, n + 1)
                if which == 0:
                    v.tensor_tensor(q_stack[64:128, par, 0, :], rotated[0:64, :], q_stack[0:64, par, 0, :],
                                    ALU.subtract)
                    v.tensor_tensor(q_stack[0:64, par, 1, :], rotated[64:128, :], q_stack[64:128, par, 1, :],
                                    ALU.subtract).then_inc(qk_low, 1)
                else:
                    for a in range(2):
                        rows = slice(64 * a, 64 * a + 64)
                        last = v.tensor_tensor(k_low[rows, par, :], rotated[rows, :], k_stack[rows, par, a, :],
                                               ALU.subtract)
                    last.then_inc(qk_low, 1)

            def pt_evac(grp, h):
                first, end = PT_GROUPS[grp]
                need(dve, pt_high, 3 * h + grp + 1)
                src = ps[:, BANK_PT + grp % 2, 0:128 * (end - first)].rearrange("p (n q) -> p n q", q=PART)
                v.tensor_tensor(pt[:, 1, first:end, :], src, pt[:, 0, first:end, :], ALU.subtract).then_inc(pt_low, 1)

            dve.wait_ge(const_in, 32)
            for t in range(ST):
                dve.wait_ge(x_in[t], 16)
                ln_stats(t, t)
            for t in range(ST):
                ln_apply(t, t)
            for t in range(ST):
                for hh in range(2):
                    xt_evac(t, hh, 0, 2 * t + hh)
            chained(v.tensor_copy(starts_f[:, :], starts_i[:, :]))
            for n in range(NSEG):
                chained(v.tensor_scalar(le[:, n, :], con[0:LR, C_TB:C_TB + TILES], starts_f[:, n:n + 1], None,
                                        ALU.is_ge))
            c0, c1, c2, c3 = (le[:, n, :] for n in range(NSEG))
            chained(v.tensor_scalar(adapter[:, :], c0, -1.0, 2.0, ALU.mult, ALU.add))
            chained(v.tensor_tensor(adapter[:, :], adapter[:, :], c1, ALU.mult))
            chained(v.tensor_tensor(c0, adapter[:, :], c0, ALU.add))
            chained(v.scalar_tensor_tensor(c3, c3, 3.0, c0, ALU.add, ALU.subtract))
            chained(v.tensor_tensor(c3, c3, c2, ALU.mult))
            chained(v.tensor_tensor(c3, c3, c0, ALU.add))
            chained(v.tensor_scalar(adapter[:, :], c3, con[0:LR, C_CODE:C_CODE + 1], None, ALU.is_equal))
            for c in range(CHUNKS):
                part_max(W_V, c)
            join_max(W_V)
            weight_scale(W_V)
            for c in range(CHUNKS):
                split_low(W_V, c)
            for c in range(CHUNKS):
                part_max(W_Q, c)
            join_max(W_Q)
            v_evac(0, 0, 0)
            weight_scale(W_Q)
            for c in range(CHUNKS):
                split_low(W_Q, c)
                if c < 2:
                    v_evac(c + 1, 0, c + 1)
            for c in range(CHUNKS):
                part_max(W_K, c)
            join_max(W_K)
            v_evac(3, 0, 3)
            weight_scale(W_K)
            chained(v.tensor_tensor(expo[:, 8:9], expo[:, W_Q:W_Q + 1], expo[:, W_K:W_K + 1], ALU.add))
            power(S_SM, expo[:, 8:9], 1, -136)
            chained(v.tensor_scalar(pow2[:, S_NEG:S_NEG + 1], pow2[:, S_SM:S_SM + 1], -1.0, None, ALU.mult))
            for c in range(CHUNKS):
                split_low(W_K, c)
            qk_drain(0, 0)
            qk_low_parts(0, 0, 0)
            qk_drain(1, 1)
            qk_low_parts(1, 0, 1)

            def head_slot(b, kind, p, a):
                first, last_b = kind == 0, kind == B - 1
                g = 16 * b + 2 * p + a
                pr = 8 * b + p
                prev = not (first and p == 0 and a == 0)
                has_qk = not (last_b and p == PAIRS - 1)
                bp = kind % 2
                if a == 0:
                    if not (first and p == 0) and not (last_b and p > 4):
                        q = (p - 1) % 8
                        v_evac(q % 4, 1 if q < 4 else 0, 3 + pr)
                    if not last_b and 1 <= p <= 4:
                        xt_evac(p - 1, 1, 1 - bp, 8 * b + 8 + 2 * p - 1)
                if prev:
                    pt_evac(0, g - 1)
                    pt_evac(1, g - 1)
                for n, j in enumerate(Q_ORDER):
                    width = 128 * (j + 1)
                    flat = ps[:, BANK_S:BANK_S + 3, :].rearrange("p b n -> p (b n)")
                    cols = slice(S_OFF[j], S_OFF[j] + width)
                    if j != 0:
                        need(dve, s_done, 3 * g + {3: 1, 2: 2, 1: 3}[j])
                    if n == 0:
                        need(dve, pt_done, 3 * g - 3)
                    v.nop(nofuse=True)
                    v.tensor_tensor_reduce(out=scores[:, a, cols], in0=flat[:, cols], in1=causal[:, 512 - width:512],
                                           scale=1.0, scalar=LOWEST, op0=ALU.add, op1=ALU.max,
                                           accum_out=row_max[:, a, j:j + 1]).then_inc(masked, 1)
                need(dve, masked, 4 * g + 4)
                v.tensor_scalar(exp_bias[:, a, :], row_max[:, a, :], pow2[:, S_NEG:S_NEG + 1], P_LOG, ALU.mult,
                                ALU.add).then_inc(bias_done, 1)
                if a == 1 and has_qk:
                    qk_drain(1, 2 * pr + 3)
                if prev:
                    pt_evac(2, g - 1)
                if a == 0 and has_qk:
                    qk_drain(0, 2 * pr + 2)
                if last_b and p in (1, 2):
                    part_max(W_O, 2 * (p - 1) + a)
                if last_b and p >= 6:
                    part_max(W_F, 2 * (p - 6) + a)
                if last_b and p == 3:
                    if a == 0:
                        join_max(W_O)
                    else:
                        weight_scale(W_O)
                        chained(v.tensor_tensor(expo[:, 9:10], expo[:, W_V:W_V + 1], expo[:, W_O:W_O + 1], ALU.add))
                        power(S_KAPPA, expo[:, 9:10], 1, -145)
                if last_b and p in (4, 5):
                    split_low(W_O, 2 * (p - 4) + a)
                if not last_b and p < 4:
                    if a == 0:
                        need(dve, x_in[p], 16 * (b + 2))
                        ln_stats(p, 4 * b + 4 + p)
                    else:
                        ln_apply(p, 4 * b + 4 + p)
                if prev:
                    h = g - 1
                    need(dve, exp_done, 4 * h + 4)
                    need(dve, o_ready, h)
                    v.reciprocal(row_inv[:, 1 - a, :], row_sum[:, 1 - a, :]).then_inc(inv_done, 1)
                    need(dve, o_copied, h + 1)
                    v.tensor_tensor(o_sum_t[:, :, :], ps_o[:, :, 0:HD], o_low[:, :, :], ALU.add).then_inc(o_added, 1)
                if has_qk:
                    qk_low_parts(a, (p + 1) % 2, 2 * pr + 2 + a)
                if a == 1 and not last_b and p < 4:
                    xt_evac(p, 0, 1 - bp, 8 * b + 8 + 2 * p)

            def batch(b, kind):
                for p in range(PAIRS):
                    for a in range(2):
                        head_slot(b, kind, p, a)

            over_batches(dve, batch)
            h = HEADS * B - 1
            for grp in range(3):
                pt_evac(grp, h)
            dve.wait_ge(exp_done, 4 * h + 4)
            dve.wait_ge(o_ready, h)
            v.reciprocal(row_inv[:, 1, :], row_sum[:, 1, :]).then_inc(inv_done, 1)
            dve.wait_ge(o_copied, h + 1)
            v.tensor_tensor(o_sum_t[:, :, :], ps_o[:, :, 0:HD], o_low[:, :, :], ALU.add).then_inc(o_added, 1)

            def low_of(grp, bank, dst, high_done, n, done):
                need(dve, high_done, n)
                ks = slice(4 * grp, 4 * grp + 4)
                v.tensor_tensor(dst[:, ks, 1, :], ps[:, bank, :].rearrange("p (k t) -> p k t", k=4),
                                dst[:, ks, 0, :], ALU.subtract).then_inc(done, 1)

            def stats(src, st, mv, bn_sem, mv_sem, n):
                for c in range(2):
                    v.bn_stats(st[:, c, :], src[c]).then_inc(bn_sem, 1)
                need(dve, bn_sem, 2 * n + 2)
                v.nop(nofuse=True)
                v.bn_aggr(mv[:, :], st[:, :, :].rearrange("p a b -> p (a b)")).then_inc(mv_sem, 1)
                need(dve, mv_sem, n + 1)

            def true_variance(sm, mv, unscale, done, n):
                v.tensor_scalar(sm[:, 3:4], mv[:, 1:2], unscale, unscale, ALU.mult, ALU.mult).then_inc(done, 1)
                need(dve, done, 2 * n + 1)
                v.tensor_scalar(sm[:, 0:1], sm[:, 3:4], EPS, None, ALU.add).then_inc(done, 1)

            def scale_and_shift(sm, mv, unscale, powered, done, n):
                need(dve, powered, n + 1)
                v.tensor_scalar(sm[:, 1:2], sm[:, 0:1], unscale, None, ALU.mult).then_inc(done, 1)
                need(dve, done, 2 * n + 1)
                v.tensor_scalar(sm[:, 2:3], mv[:, 0:1], sm[:, 1:2], -1.0, ALU.mult, ALU.mult).then_inc(done, 1)

            kappa = pow2[:, S_KAPPA:S_KAPPA + 1]
            kf = pow2[:, S_KF:S_KF + 1]
            dve.wait_ge(pv_done, HEADS * B)
            chained(v.memset(b_raw, 0.0))
            chained(v.memset(b_split[:, 1, :], 0.0))
            chained(v.memset(t_stack, 0.0))
            chained(v.memset(t_stack[32:64, :], ONE))
            v.tensor_scalar(pow2[:, S_NOTBIAS:S_NOTBIAS + 1], con[:, C_BIASROW:C_BIASROW + 1], -1.0, 1.0, ALU.mult,
                            ALU.add).then_inc(lora_ready, 1)
            for grp in range(2):
                low_of(grp, BANK_TR + grp, o_t, ot_high, grp + 1, ot_low)
            join_max(W_F)
            dve.wait_ge(lora_ready, 1)
            dve.wait_ge(lora_in, 64)
            chained(v.tensor_reduce(w_pmax[:, 5:6], a_raw, AX.XY, ALU.max, apply_absolute_value=True))
            chained(v.tensor_reduce(field[:, 1:2], b_raw, AX.X, ALU.max, apply_absolute_value=True))
            chained(v.tensor_tensor(w_pmax[:, 6:7], field[:, 1:2], pow2[:, S_NOTBIAS:S_NOTBIAS + 1], ALU.mult))
            v.tensor_tensor(w_pmax[:, 7:8], field[:, 1:2], con[:, C_BIASROW:C_BIASROW + 1],
                            ALU.mult).then_inc(pmax_done, 1)
            dve.wait_ge(max_done, W_F + 1)
            exponents(4, 4)
            chained(v.tensor_tensor(expo[:, 10:11], expo[:, 5:6], expo[:, 6:7], ALU.add))
            chained(v.tensor_scalar(expo[:, 10:11], expo[:, 10:11], -121.0, None, ALU.add))
            chained(v.tensor_scalar(expo[:, 11:12], expo[:, 7:8], -4.0, None, ALU.add))
            chained(v.tensor_tensor(expo[:, 11:12], expo[:, 11:12], expo[:, 10:11], ALU.max))
            chained(v.tensor_tensor(expo[:, 11:12], expo[:, 11:12], expo[:, 4:5], ALU.max))
            power(W_F, expo[:, 11:12], -1, 268)
            v.tensor_copy(pow2[:, 15:16], pow2[:, W_F:W_F + 1]).then_inc(scale_done, 1)
            power(S_A, expo[:, 5:6], -1, 268)
            chained(v.tensor_tensor(expo[:, 10:11], expo[:, 5:6], expo[:, 11:12], ALU.subtract))
            power(S_B, expo[:, 10:11], 1, 147)
            power(S_BIAS, expo[:, 11:12], -1, 264)
            power(S_KF, expo[:, 11:12], 1, -24)
            chained(v.tensor_tensor(pow2[:, S_B:S_B + 1], pow2[:, S_B:S_B + 1], pow2[:, S_NOTBIAS:S_NOTBIAS + 1],
                                    ALU.mult))
            chained(v.tensor_tensor(pow2[:, S_BIAS:S_BIAS + 1], pow2[:, S_BIAS:S_BIAS + 1],
                                    con[:, C_BIASROW:C_BIASROW + 1], ALU.mult))
            chained(v.tensor_tensor(pow2[:, S_ROWS:S_ROWS + 1], pow2[:, S_B:S_B + 1], pow2[:, S_BIAS:S_BIAS + 1],
                                    ALU.add))
            chained(v.tensor_scalar(a_split[:, :, 0, :], a_raw, pow2[:, S_A:S_A + 1], None, ALU.mult))
            chained(v.scalar_tensor_tensor(a_split[:, :, 1, :], a_raw, pow2[:, S_A:S_A + 1], a_split[:, :, 0, :],
                                           ALU.mult, ALU.subtract))
            chained(v.tensor_scalar(b_split[:, 0, :], b_raw, pow2[:, S_ROWS:S_ROWS + 1], None, ALU.mult))
            v.scalar_tensor_tensor(b_split[0:LOW_ROW, 1, :], b_raw[0:LOW_ROW, :], pow2[0:LOW_ROW, S_ROWS:S_ROWS + 1],
                                   b_split[0:LOW_ROW, 0, :], ALU.mult, ALU.subtract).then_inc(lora_ready, 1)
            for c in range(CHUNKS):
                split_low(W_F, c)

            ps_ff = [ps[:, BANK_FF + c, :] for c in range(2)]
            ps_ao = [ps[:, BANK_AO + c, :] for c in range(2)]

            def step(i, kind, i2):
                a = kind % 2
                if kind >= 2:
                    need(dve, ff_done, i - 1)
                    stats(ps_ff, st2, mv2, bn2_done, mv2_done, i - 2)
                    true_variance(sm2, mv2, kf, var2_done, i - 2)
                if 1 <= kind <= TILES:
                    for grp in range(2):
                        low_of(grp, BANK_TR + grp, xn2_t, x2t_high, 2 * i - 1 + grp, x2t_low)
                if kind >= 2:
                    scale_and_shift(sm2, mv2, kf, pow2_done, rm2_done, i - 2)
                    need(dve, u2_done, i - 1)
                    need(dve, y_stored[a], 16 * (i2 - 1))
                    v.tensor_tensor(y_out[:, a], x2[:, a], u2, ALU.add).then_inc(y_done, 1)
                if kind < TILES:
                    need(dve, ao_done, i + 1)
                    stats(ps_ao, st1, mv1, bn1_done, mv1_done, i)
                    true_variance(sm1, mv1, kappa, var1_done, i)
                if 1 <= kind <= TILES:
                    need(dve, lt_done, i)
                    v.tensor_scalar(t_f, ps[0:LR, BANK_T, 0:128], T_DOWN, adapter[:, bass.ds(i - 1, 1)], ALU.mult,
                                    ALU.mult).then_inc(lt_scaled, 1)
                    need(dve, lt_scaled, i)
                    v.tensor_copy(t_stack[0:LR, :], t_f).then_inc(lt_high, 1)
                    need(dve, lt_high, i)
                    v.tensor_tensor(t_stack[LOW_ROW:LOW_ROW + LR, :], t_f, t_stack[0:LR, :],
                                    ALU.subtract).then_inc(lt_low, 1)
                if kind < TILES:
                    scale_and_shift(sm1, mv1, kappa, pow1_done, rm1_done, i)
                if kind <= TILES - 2:
                    for grp in range(2):
                        low_of(grp, BANK_TR + grp, o_t, ot_high, 2 * i + 3 + grp, ot_low)
                if kind < TILES:
                    need(dve, u1_done, i + 1)
                    need(dve, x_tile_in[a], 16 * (i2 + 1))
                    v.tensor_tensor(x2[:, a], x2[:, a], u1, ALU.add).then_inc(x2_done, 1)
                    need(dve, x2_done, i + 1)
                    stats([x2[:, a, 512 * c:512 * c + 512] for c in range(2)], stx, mvx, bnx_done, mvx_done, i)
                    v.tensor_scalar(smx[:, 0:1], mvx[:, 1:2], EPS, XS2, ALU.add, ALU.mult).then_inc(varx_done, 1)
                    need(dve, powx_done, i + 1)
                    v.tensor_scalar(xn2, x2[:, a], mvx[:, 0:1], smx[:, 1:2], ALU.subtract,
                                    ALU.mult).then_inc(xn2_done, 1)

            over_tiles(dve, step)

        @block.scalar
        def _(act):
            s = nc.scalar

            def split_high(w, c):
                act.wait_ge(scale_done, w + 1)
                act.wait_ge(raw_in[w][c], 16)
                ks = slice(KC * c, KC * (c + 1))
                s.activation(w_dst[w][:, ks, 0, :], w_raw[w][:, ks, :], ACT.Copy,
                             scale=pow2[:, w:w + 1]).then_inc(w_high_done, 1)

            def xt_evac(t, hh, par, n):
                need(act, xt_done, n + 1)
                dst = xnt[par][:, 4 * hh:4 * hh + 4, 0, 128 * t:128 * t + 128]
                s.activation(dst, ps[:, BANK_K, :].rearrange("p (k t) -> p k t", k=4),
                             ACT.Copy).then_inc(xt_high, 1)

            def v_evac(t, h8, n):
                need(act, v_done, n + 1)
                s.activation(v_split[:, t, 8 * h8:8 * h8 + 8, 0:HD],
                             ps[:, BANK_Q, :].rearrange("p (h c) -> p h c", h=8), ACT.Copy,
                             scale=V_DOWN).then_inc(v_high, 1)

            def qk_high_parts(which, par, n):
                need(act, rot_done, n + 1)
                dsts = [(0, q_stack[0:64, par, 0, :]), (1, q_stack[64:128, par, 1, :])] if which == 0 else [
                    (a, k_stack[64 * r:64 * r + 64, par, a, :]) for a in range(2) for r in range(2)]
                for a, dst in dsts:
                    last = s.activation(dst, rotated[64 * a:64 * a + 64, :], ACT.Copy)
                last.then_inc(qk_high, 1)

            def pt_evac(grp, h):
                first, end = PT_GROUPS[grp]
                need(act, pt_done, 3 * h + grp + 1)
                src = ps[:, BANK_PT + grp % 2, 0:128 * (end - first)].rearrange("p (n q) -> p n q", q=PART)
                s.activation(pt[:, 0, first:end, :], src, ACT.Copy).then_inc(pt_high, 1)

            def o_copy(h):
                need(act, pv_done, h + 1)
                need(act, o_added, h)
                s.activation(o_low[:, :, :], ps_o[:, :, HD:2 * HD], ACT.Copy).then_inc(o_copied, 1)

            for t in range(ST):
                for hh in range(2):
                    xt_evac(t, hh, 0, 2 * t + hh)
            for c in range(CHUNKS):
                split_high(W_V, c)
            v_evac(0, 0, 0)
            for c in range(CHUNKS):
                split_high(W_Q, c)
                if c < 2:
                    v_evac(c + 1, 0, c + 1)
            v_evac(3, 0, 3)
            for c in range(CHUNKS):
                if c == 0:
                    act.wait_ge(w_low_done, CHUNKS * (W_Q + 1))
                split_high(W_K, c)
            qk_high_parts(0, 0, 0)
            qk_high_parts(1, 0, 1)

            def head_slot(b, kind, p, a):
                first, last_b = kind == 0, kind == B - 1
                g = 16 * b + 2 * p + a
                pr = 8 * b + p
                prev = not (first and p == 0 and a == 0)
                bp = kind % 2
                if a == 0:
                    if not (first and p == 0) and not (last_b and p > 4):
                        q = (p - 1) % 8
                        v_evac(q % 4, 1 if q < 4 else 0, 3 + pr)
                    if not last_b and 1 <= p <= 4:
                        xt_evac(p - 1, 1, 1 - bp, 8 * b + 8 + 2 * p - 1)
                if prev:
                    for grp in range(3):
                        pt_evac(grp, g - 1)
                need(act, bias_done, g + 1)
                for j in Q_ORDER:
                    cols = slice(S_OFF[j], S_OFF[j] + 128 * (j + 1))
                    s.activation(scores[:, a, cols], scores[:, a, cols], ACT.Exp, bias=exp_bias[:, a, j:j + 1],
                                 scale=pow2[:, S_SM:S_SM + 1],
                                 accum_out=row_sum[:, a, j:j + 1]).then_inc(exp_done, 1)
                if last_b and p in (4, 5):
                    if p == 4 and a == 0:
                        act.wait_ge(v_done, 8 * B)
                    split_high(W_O, 2 * (p - 4) + a)
                if prev:
                    o_copy(g - 1)
                if not (last_b and p == PAIRS - 1):
                    qk_high_parts(a, (p + 1) % 2, 2 * pr + 2 + a)
                if a == 1 and not last_b and p < 4:
                    xt_evac(p, 0, 1 - bp, 8 * b + 8 + 2 * p)

            def batch(b, kind):
                for p in range(PAIRS):
                    for a in range(2):
                        head_slot(b, kind, p, a)

            over_batches(act, batch)
            for grp in range(3):
                pt_evac(grp, HEADS * B - 1)
            o_copy(HEADS * B - 1)

            def high_of(grp, bank, dst, made, n, done):
                need(act, made, n)
                s.activation(dst[:, 4 * grp:4 * grp + 4, 0, :], ps[:, bank, :].rearrange("p (k t) -> p k t", k=4),
                             ACT.Copy).then_inc(done, 1)

            def normalise(u, bank, sm, ready, n, done):
                need(act, ready, 2 * n + 2)
                s.activation(u.rearrange("p (c n) -> p c n", c=2), ps[:, bank:bank + 2, :], ACT.Identity,
                             bias=sm[:, 2:3], scale=sm[:, 1:2]).then_inc(done, 1)

            for grp in range(2):
                high_of(grp, BANK_TR + grp, o_t, ot_done, grp + 1, ot_high)
            for c in range(CHUNKS):
                split_high(W_F, c)

            def step(i, kind, i2):
                if 1 <= kind <= TILES:
                    for grp in range(2):
                        high_of(grp, BANK_TR + grp, xn2_t, x2t_done, 2 * i - 1 + grp, x2t_high)
                if kind >= 2:
                    need(act, y_done, i - 2)
                    normalise(u2, BANK_FF, sm2, rm2_done, i - 2, u2_done)
                if kind <= TILES - 2:
                    need(act, ao_done, i + 1)
                    for grp in range(2):
                        high_of(grp, BANK_TR + grp, o_t, ot_done, 2 * i + 3 + grp, ot_high)
                if kind < TILES:
                    need(act, x2_done, i)
                    normalise(u1, BANK_AO, sm1, rm1_done, i, u1_done)

            over_tiles(act, step)

        @block.gpsimd
        def _(pool):
            gp = nc.gpsimd
            minus_half = con[:, C_HALF:C_HALF + 1]

            def weight_max(w, n):
                pool.wait_ge(pmax_done, w + 1 + (1 if w == W_F else 0))
                gp.partition_all_reduce(w_max[:, w:w + n], w_pmax[:, w:w + n], PART, ABSMAX).then_inc(max_done, 1)

            def ln_rstd(t, n):
                need(pool, var_done, n + 1)
                gp.tensor_tensor(rstd[:, t:t + 1], var_s[:, t:t + 1], minus_half, ALU.pow).then_inc(rstd_done, 1)

            def rotate(n):
                need(pool, qk_drained, n + 1)
                gp.tensor_tensor(swapped[:, :], swapped[:, :], sin_t, ALU.mult).then_inc(rot_mul, 1)
                need(pool, rot_mul, n + 1)
                gp.tensor_tensor(rotated[:, :], rotated[:, :], swapped[:, :], ALU.add).then_inc(rot_done, 1)

            def o_scale(h, a, p, stored):
                need(pool, o_added, h + 1)
                need(pool, inv_done, h + 1)
                if a == 0:
                    need(pool, o_stored[p % 2], stored)
                gp.tensor_tensor(o_pair[:, p % 2, :, 64 * a:64 * a + 64], o_sum_t[:, :, :],
                                 row_inv[:, a, :].unsqueeze(2).broadcast_to([PART, ST, HD]),
                                 ALU.mult).then_inc(o_ready, 1)

            pool.wait_ge(const_in, 32)
            for t in range(ST):
                ln_rstd(t, t)
            for w in (W_V, W_Q, W_K):
                weight_max(w, 1)
            rotate(0)
            rotate(1)

            def batch(b, kind):
                first, last_b = kind == 0, kind == B - 1
                for p in range(PAIRS):
                    for a in range(2):
                        g = 16 * b + 2 * p + a
                        pr = 8 * b + p
                        if last_b and p == 3 and a == 0:
                            weight_max(W_O, 1)
                        if a == 1 and not (last_b and p == PAIRS - 1):
                            rotate(2 * pr + 3)
                        if a == 0 and not (last_b and p == PAIRS - 1):
                            rotate(2 * pr + 2)
                        if not last_b and p < 4 and a == 0:
                            ln_rstd(p, 4 * b + 4 + p)
                        if not (first and p == 0 and a == 0):
                            if a == 1:
                                o_scale(g - 1, 0, p, 16 * (4 * b + p // 2))
                            else:
                                o_scale(g - 1, 1, p - 1, 0)

            over_batches(pool, batch)
            o_scale(HEADS * B - 1, 1, PAIRS - 1, 0)
            weight_max(W_F, 4)

            def power_half(sm, out_col, ready, n, done):
                need(pool, ready, n)
                gp.tensor_tensor(sm[:, out_col:out_col + 1], sm[:, 0:1], minus_half, ALU.pow).then_inc(done, 1)

            def step(i, kind, i2):
                if kind >= 2:
                    power_half(sm2, 0, var2_done, 2 * (i - 2) + 2, pow2_done)
                if kind < TILES:
                    power_half(sm1, 0, var1_done, 2 * i + 2, pow1_done)
                    power_half(smx, 1, varx_done, i + 1, powx_done)

            over_tiles(pool, step)


def _constants():
    import numpy as np

    c = np.zeros((PART, C_LEN), np.float32)
    c[:, C_ID:C_ID + 128] = np.eye(128, dtype=np.float32)
    r = np.arange(PART)
    c[:, C_MASK + 384:C_MASK + 512] = np.where(r[None, :] > r[:, None], np.float32(NEG), np.float32(0))
    inv_freq = np.float32(1) / (np.float32(10000) ** (np.arange(0, HD, 2, dtype=np.float32) / np.float32(HD)))
    angle = np.arange(S, dtype=np.float32)[None, :] * inv_freq[(r % HD) // 2][:, None]
    c[:, C_COS:C_COS + S] = np.cos(angle.astype(np.float64)).astype(np.float32) * np.float32(QK_DOWN)
    c[:, C_SIN:C_SIN + S] = np.sin(angle.astype(np.float64)).astype(np.float32) * np.float32(QK_DOWN)
    c[LR, C_BIASROW] = 1
    c[:, C_TB:C_TB + TILES] = np.arange(TILES) // ST
    c[:LR, C_CODE] = np.arange(LR) // RANK + 2
    c[:, C_HALF:C_HALF + 4] = -0.5
    return c


def kernel(**inputs):
    import numpy as _np
    import concourse.bacc as _bacc
    from concourse import mybir as _mybir
    from concourse.bass_utils import run_bass_kernel_spmd as _run

    a = {k: _np.asarray(v) for k, v in inputs.items()}
    lora_b = a["L0_ffn_lora_B"]
    arrays = {
        "x": a["L0_attn_hidden_states"],
        "wq": a["L0_attn_Wq"],
        "wk": a["L0_attn_Wk"],
        "wv": a["L0_attn_Wv"],
        "wo": a["L0_attn_Wo"],
        "wf": a["L0_ffn_weight"].T,
        "bias": a["L0_ffn_bias"].reshape(1, D),
        "lora_a": a["L0_ffn_lora_A"].reshape(LR, D).T,
        "lora_b": lora_b.transpose(0, 2, 1).reshape(LR, D),
        "starts": _np.broadcast_to(a["L0_ffn_lora_start_indices"].reshape(1, NSEG), (LR, NSEG)),
        "consts": _constants(),
    }
    arrays = {k: _np.ascontiguousarray(v) for k, v in arrays.items()}
    nc = _bacc.Bacc("TRN2", target_bir_lowering=False, num_devices=1)
    args = [nc.dram_tensor(k, v.shape, _mybir.dt.from_np(v.dtype), kind="ExternalInput").ap()
            for k, v in arrays.items()]
    out = nc.dram_tensor("out", (B, S, D), F32, kind="ExternalOutput").ap()
    sandwich_kernel(nc, *args, out)
    r = _run(nc, [arrays], core_ids=[0])
    return r.results[0]["out"]
```

```python
from contextlib import ExitStack

import concourse.bass as bass
from concourse import mybir

ALU = mybir.AluOpType
ACT = mybir.ActivationFunctionType
AX = mybir.AxisListType
F32 = mybir.dt.float32
F16 = mybir.dt.float16
I32 = mybir.dt.int32
ABSMAX = bass.bass_isa.ReduceOp.absmax

PART = 128
B, S, D = 8, 512, 1024
HEADS, HD = 16, 64
KT = D // PART
ST = S // PART
PAIRS = HEADS // 2
TILES = B * ST
NLORA, RANK, NSEG = 3, 16, 4
LR = NLORA * RANK
LOW_ROW = 64
CHUNKS, KC = 4, KT // 4

EPS = 1e-5
XS = 2.0 ** 10
XS2 = XS ** -2
V_DOWN = 2.0 ** -20
QK_DOWN = 2.0 ** -21
T_DOWN = 2.0 ** -20
ONE = 2.0 ** 14
P_LOG = 9.704060527839234
NEG = -1e30
LOWEST = -3e38

Q_ORDER = (3, 2, 0, 1)
S_OFF = {3: 0, 2: 512, 0: 896, 1: 1024}
S_LEN = 1280
BLOCKS = [(j, kt) for j in Q_ORDER for kt in range(j + 1)]
PT_GROUPS = ((0, 4), (4, 8), (8, 10))
PT_PLACE = ((5, 0), (6, 0), (4, 256))

BANK_Q, BANK_K, BANK_S, BANK_O = 0, 1, 2, 7
FIRST_XT, FIRST_V = (1, 2, 3), (0, 2, 0, 7)
BANK_SQUARES = 4
BANK_FF, BANK_AO, BANK_T, BANK_TR = 0, 2, 4, 5

C_ID = 0
C_MASK = C_ID + 128
C_COS = C_MASK + 512
C_SIN = C_COS + 512
C_BIASROW = C_SIN + 512
C_TB = C_BIASROW + 1
C_CODE = C_TB + TILES
C_HALF = C_CODE + 1
C_LEN = C_HALF + 4

W_V, W_Q, W_K, W_O, W_F = range(5)


def sandwich_kernel(nc, x, wq, wk, wv, wo, wf, bias, lora_a, lora_b, starts, consts, out):
    x_v = x.rearrange("b (t p) d -> b t p d", p=PART)
    x_tiles = x.rearrange("b (t p) d -> (b t) p d", p=PART)
    out_tiles = out.rearrange("b (t p) d -> (b t) p d", p=PART)
    raw_dram = [w.rearrange("(k p) n -> p k n", p=PART) for w in (wv, wq, wk, wo, wf)]
    a_dram = lora_a.rearrange("(k p) r -> p k r", p=PART)
    attn = nc.dram_tensor("attn_scratch", (B * S, D), F32, kind="Internal").ap()
    attn_pairs = attn.rearrange("(b t p) (h c) -> b h p t c", b=B, p=PART, h=PAIRS)
    attn_tiles = attn.rearrange("(i p) d -> i p d", p=PART)

    with ExitStack() as ctx:
        def sb(name, shape, dt):
            return ctx.enter_context(nc.sbuf_tensor(name, shape, dt))

        def sem(name):
            return ctx.enter_context(nc.semaphore(name))

        region = [sb(f"region{i}", [PART, KT, 2, D], F16) for i in range(3)]
        w_dst = {W_V: region[2], W_Q: region[0], W_K: region[1], W_O: region[2], W_F: region[0]}
        arena1 = sb("arena1", [PART, 9216], F32)
        arena2 = sb("arena2", [PART, 8192], F32)
        raw1 = arena1[:, 0:8192].rearrange("p (k n) -> p k n", k=KT)
        raw2 = arena2[:, :].rearrange("p (k n) -> p k n", k=KT)
        raw_r1 = region[1][:, :, :, :].rearrange("p k h n -> p (k h n)").bitcast(F32).rearrange(
            "p (k n) -> p k n", k=KT)
        w_raw = {W_V: raw1, W_Q: raw_r1, W_K: raw1, W_O: raw2, W_F: raw2}

        x_ring = arena2[:, 0:4096].rearrange("p (t d) -> p t d", t=ST)

        def half(ap, shape):
            return ap.bitcast(F16).rearrange(shape[0], **shape[1])

        xnt_shape = ("p (k h t) -> p k h t", dict(k=KT, h=2))
        xnt = [half(arena2[:, 4096:8192], xnt_shape), half(arena1[:, 0:4096], xnt_shape)]
        scores = arena1[:, 4096:4096 + 2 * S_LEN].rearrange("p (a n) -> p a n", a=2)
        pt = half(arena1[:, 6656:6656 + S_LEN], ("p (h n q) -> p h n q", dict(h=2, q=PART)))
        o_pair = arena1[:, 7936:7936 + 1024].rearrange("p (a t c) -> p a t c", a=2, t=ST)

        v_split = sb("v_split", [PART, ST, HEADS, 2 * HD], F16)
        q_stack = sb("q_stack", [PART, 2, 2, S], F16)
        k_stack = sb("k_stack", [PART, 2, 2, S], F16)
        k_low = sb("k_low", [PART, 2, S], F16)
        swapped = sb("swapped", [PART, S], F32)
        rotated = sb("rotated", [PART, S], F32)
        o_low = sb("o_low", [PART, ST, HD], F32)
        o_sum_t = sb("o_sum_t", [PART, ST, HD], F32)
        con = sb("con", [PART, C_LEN], F32)
        ident = con[:, C_ID:C_ID + 128]
        causal = con[:, C_MASK:C_MASK + 512]
        cos_t = con[:, C_COS:C_COS + 512]
        sin_t = con[:, C_SIN:C_SIN + 512]
        row_max = sb("row_max", [PART, 2, ST], F32)
        exp_bias = sb("exp_bias", [PART, 2, ST], F32)
        row_sum = sb("row_sum", [PART, 2, ST], F32)
        row_inv = sb("row_inv", [PART, 2, ST], F32)
        bn = sb("bn", [PART, ST, 2, 6], F32)
        mean_var = sb("mean_var", [PART, ST, 2], F32)
        var_s = sb("var_s", [PART, ST], F32)
        rstd = sb("rstd", [PART, ST], F32)
        w_part = sb("w_part", [PART, 5, CHUNKS], F32)
        w_pmax = sb("w_pmax", [PART, 8], F32)
        w_max = sb("w_max", [PART, 8], F32)
        expo_i = sb("expo_i", [PART, 8], I32)
        expo = sb("expo", [PART, 12], F32)
        field = sb("field", [PART, 2], F32)
        field_i = sb("field_i", [PART, 1], I32)
        pow2 = sb("pow2", [PART, 16], F32)
        S_SM, S_NEG, S_KAPPA, S_A, S_B, S_BIAS, S_KF, S_ROWS, S_NOTBIAS = range(5, 14)
        starts_i = sb("starts_i", [LR, NSEG], I32)
        starts_f = sb("starts_f", [LR, NSEG], F32)
        le = sb("le", [LR, NSEG, TILES], F32)
        adapter = sb("adapter", [LR, TILES], F32)

        r1f = region[1][:, :, :, :].rearrange("p k h n -> p (k h n)").bitcast(F32)
        o_in = r1f[:, 0:2048].rearrange("p (a d) -> p a d", a=2)
        x2 = r1f[:, 2048:4096].rearrange("p (a d) -> p a d", a=2)
        y_out = r1f[:, 4096:6144].rearrange("p (a d) -> p a d", a=2)
        o_t = half(r1f[:, 6144:7168], ("p (k h t) -> p k h t", dict(k=KT, h=2)))
        xn2_t = half(r1f[:, 7168:8192], ("p (k h t) -> p k h t", dict(k=KT, h=2)))
        b_raw = arena1[:, 0:1024]
        b_split = half(arena1[:, 1024:2048], ("p (h n) -> p h n", dict(h=2)))
        a_raw = arena1[:, 2048:2048 + KT * LR].rearrange("p (k r) -> p k r", k=KT)
        a_split = half(arena1[:, 2432:2432 + KT * LR], ("p (k h r) -> p k h r", dict(k=KT, h=2)))
        t_f = arena1[0:LR, 2816:2944]
        t_stack = arena1[:, 2944:3008].bitcast(F16)
        u1 = arena1[:, 4096:5120]
        u2 = arena1[:, 5120:6144]
        xn2 = arena1[:, 6144:7168]

        ps = ctx.enter_context(nc.psum_tensor("ps", [PART, 8, 512], F32))
        ps_o = ps[:, BANK_O, :].rearrange("p (t c) -> p t c", t=ST)

        const_in = sem("const_in")
        raw_in = [[sem(f"raw_in_{w}_{c}") for c in range(CHUNKS)] for w in range(5)]
        x_in = [sem(f"x_in{t}") for t in range(ST)]
        lora_in = sem("lora_in")
        o_stored = [sem(f"o_stored{a}") for a in range(2)]
        part_max_done = sem("part_max_done")
        squares_done = sem("squares_done")
        pmax_done = sem("pmax_done")
        max_done = sem("max_done")
        scale_done = sem("scale_done")
        w_high_done = sem("w_high_done")
        w_low_done = sem("w_low_done")
        dve_step = sem("dve_step")
        bn_done = sem("bn_done")
        meanvar_done = sem("meanvar_done")
        var_done = sem("var_done")
        rstd_done = sem("rstd_done")
        xn_done = sem("xn_done")
        xt_done = sem("xt_done")
        xt_high = sem("xt_high")
        xt_low = sem("xt_low")
        qk_done = sem("qk_done")
        qk_drained = sem("qk_drained")
        rot_mul = sem("rot_mul")
        rot_done = sem("rot_done")
        qk_high = sem("qk_high")
        qk_low = sem("qk_low")
        v_done = sem("v_done")
        v_high = sem("v_high")
        v_low = sem("v_low")
        s_done = sem("s_done")
        masked = sem("masked")
        bias_done = sem("bias_done")
        exp_done = sem("exp_done")
        pt_done = sem("pt_done")
        pt_high = sem("pt_high")
        pt_low = sem("pt_low")
        pv_done = sem("pv_done")
        o_copied = sem("o_copied")
        o_added = sem("o_added")
        inv_done = sem("inv_done")
        o_ready = sem("o_ready")
        o_tile_in = [sem(f"o_tile_in{a}") for a in range(2)]
        x_tile_in = [sem(f"x_tile_in{a}") for a in range(2)]
        y_stored = [sem(f"y_stored{a}") for a in range(2)]
        ot_done = sem("ot_done")
        ot_high = sem("ot_high")
        ot_low = sem("ot_low")
        ao_done = sem("ao_done")
        bn1_done = sem("bn1_done")
        mv1_done = sem("mv1_done")
        var1_done = sem("var1_done")
        pow1_done = sem("pow1_done")
        rm1_done = sem("rm1_done")
        u1_done = sem("u1_done")
        x2_done = sem("x2_done")
        bnx_done = sem("bnx_done")
        mvx_done = sem("mvx_done")
        varx_done = sem("varx_done")
        powx_done = sem("powx_done")
        xn2_done = sem("xn2_done")
        x2t_done = sem("x2t_done")
        x2t_high = sem("x2t_high")
        x2t_low = sem("x2t_low")
        lt_done = sem("lt_done")
        lt_scaled = sem("lt_scaled")
        lt_high = sem("lt_high")
        lt_low = sem("lt_low")
        lora_ready = sem("lora_ready")
        ff_done = sem("ff_done")
        bn2_done = sem("bn2_done")
        mv2_done = sem("mv2_done")
        var2_done = sem("var2_done")
        pow2_done = sem("pow2_done")
        rm2_done = sem("rm2_done")
        u2_done = sem("u2_done")
        y_done = sem("y_done")

        mv1 = sb("mv1", [PART, 2], F32)
        st1 = sb("st1", [PART, 2, 6], F32)
        sm1 = sb("sm1", [PART, 4], F32)
        mvx = sb("mvx", [PART, 2], F32)
        stx = sb("stx", [PART, 2, 6], F32)
        smx = sb("smx", [PART, 2], F32)
        mv2 = sb("mv2", [PART, 2], F32)
        st2 = sb("st2", [PART, 2, 6], F32)
        sm2 = sb("sm2", [PART, 4], F32)

        def need(eng, semaphore, count):
            if isinstance(count, int) and count <= 0:
                return
            eng.wait_ge(semaphore, count)

        def over_batches(eng, body):
            body(0, 0)
            with eng.Fori(0, (B - 2) // 2) as it:
                body(2 * it + 1, 1)
                body(2 * it + 2, 2)
            body(B - 1, B - 1)

        def over_tiles(eng, body):
            for i in range(4):
                body(i, i, i // 2)
            with eng.Fori(0, (TILES - 6) // 2) as it:
                body(2 * it + 4, 4, it + 2)
                body(2 * it + 5, 5, it + 2)
            for i in range(TILES - 2, TILES + 2):
                body(i, i, i // 2)

        block = ctx.enter_context(nc.Block())

        @block.sync
        def _(sp):
            def load_raw(w, c):
                sp.dma_start(w_raw[w][:, KC * c:KC * (c + 1), :],
                             raw_dram[w][:, KC * c:KC * (c + 1), :]).then_inc(raw_in[w][c], 16)

            for t in range(ST):
                sp.dma_start(x_ring[:, t, :], x_v[0, t]).then_inc(x_in[t], 16)
            sp.dma_start(con[:, :], consts).then_inc(const_in, 16)
            sp.dma_start(starts_i[:, :], starts).then_inc(const_in, 16)
            for w in (W_V, W_Q):
                for c in range(CHUNKS):
                    load_raw(w, c)
            for c in range(CHUNKS):
                sp.wait_ge(w_low_done, CHUNKS * W_V + c + 1)
                load_raw(W_K, c)

            def load_tile(i, a):
                sp.dma_start(o_in[:, a], attn_tiles[i]).then_inc(o_tile_in[a], 16)

            def phase2_loads():
                sp.wait_ge(lora_ready, 1)
                sp.wait_ge(qk_done, 2 * PAIRS * B)
                sp.dma_start(a_raw, a_dram).then_inc(lora_in, 16)
                sp.dma_start(b_raw[0:LR, :], lora_b).then_inc(lora_in, 16)
                sp.dma_start(b_raw[LOW_ROW:LOW_ROW + LR, :], lora_b).then_inc(lora_in, 16)
                sp.dma_start(b_raw[LR:LR + 1, :], bias).then_inc(lora_in, 16)
                for a in range(2):
                    sp.wait_ge(o_stored[a], 16 * PAIRS // 2)
                load_tile(0, 0)
                load_tile(1, 1)

            def batch(b, kind):
                if kind < B - 1:
                    for t in range(ST):
                        sp.wait_ge(xt_done, 8 * b + 2 * t + 2)
                        sp.dma_start(x_ring[:, t, :], x_v[b + 1, t]).then_inc(x_in[t], 16)
                else:
                    sp.wait_ge(xt_done, 8 * B)
                    sp.wait_ge(qk_done, 2 * PAIRS * (B - 1))
                    sp.wait_ge(v_done, 8 * (B - 1))
                    for c in range(CHUNKS):
                        load_raw(W_O, c)
                if kind > 0:
                    sp.wait_ge(o_ready, 16 * b)
                    sp.dma_start(attn_pairs[b - 1, PAIRS - 1], o_pair[:, 1]).then_inc(o_stored[1], 16)
                for p in range(PAIRS - 1):
                    if kind == B - 1 and p == 5:
                        for c in range(CHUNKS):
                            sp.wait_ge(w_low_done, CHUNKS * W_O + c + 1)
                            load_raw(W_F, c)
                    if kind == B - 1 and p == 6:
                        phase2_loads()
                    sp.wait_ge(o_ready, 16 * b + 2 * p + 2)
                    sp.dma_start(attn_pairs[b, p], o_pair[:, p % 2]).then_inc(o_stored[p % 2], 16)

            over_batches(sp, batch)

            sp.wait_ge(o_ready, HEADS * B)
            sp.dma_start(attn_pairs[B - 1, PAIRS - 1], o_pair[:, 1]).then_inc(o_stored[1], 16)
            for a in range(2):
                sp.wait_ge(o_stored[a], 16 * PAIRS * B // 2)
            def step(i, kind, i2):
                a = kind % 2
                if kind >= 2:
                    if kind < TILES:
                        sp.wait_ge(y_done, i - 1)
                if kind < TILES:
                    sp.dma_start(x2[:, a], x_tiles[i]).then_inc(x_tile_in[a], 16)
                if kind <= TILES - 3:
                    sp.wait_ge(ot_done, 2 * i + 2)
                    load_tile(i + 2, a)
                if kind >= 2:
                    sp.wait_ge(y_done, i - 1)
                    sp.dma_start(out_tiles[i - 2], y_out[:, a]).then_inc(y_stored[a], 16)

            over_tiles(sp, step)
            for a in range(2):
                sp.wait_ge(y_stored[a], 16 * TILES // 2)

        @block.tensor
        def _(pe):
            mm = nc.tensor.matmul

            def x_transposes(ring_t, hh, drained, bank=BANK_K):
                need(pe, xt_low, drained)
                for k in range(4):
                    last = nc.tensor.transpose(ps[:, bank, 128 * k:128 * k + 128],
                                               x_ring[:, ring_t, 512 * hh + 128 * k:512 * hh + 128 * k + 128],
                                               ident)
                last.then_inc(xt_done, 1)

            def qk_product(which, pair, par, ks):
                w, bank = region[which], (BANK_Q, BANK_K)[which]
                cols = slice(128 * pair, 128 * pair + 128)
                for k in ks:
                    o = ps[:, bank, :]
                    mm(o, w[:, k, 0, cols], xnt[par][:, k, 0, :], start=(k == 0), stop=False)
                    mm(o, w[:, k, 0, cols], xnt[par][:, k, 1, :], start=False, stop=False)
                    last = mm(o, w[:, k, 1, cols], xnt[par][:, k, 0, :], start=False, stop=(k == KT - 1))
                if ks[-1] == KT - 1:
                    last.then_inc(qk_done, 1)

            def v_product(t, h8, par, ks, bank=BANK_Q):
                cols = slice(512 * h8, 512 * h8 + 512)
                tok = slice(128 * t, 128 * t + 128)
                for k in ks:
                    o = ps[:, bank, :]
                    mm(o, xnt[par][:, k, 0, tok], region[2][:, k, 0, cols], start=(k == 0), stop=False)
                    mm(o, xnt[par][:, k, 0, tok], region[2][:, k, 1, cols], start=False, stop=False)
                    last = mm(o, xnt[par][:, k, 1, tok], region[2][:, k, 0, cols], start=False, stop=(k == KT - 1))
                if ks[-1] == KT - 1:
                    last.then_inc(v_done, 1)

            def pt_group(g, a):
                first, end = PT_GROUPS[g]
                bank, col = PT_PLACE[g]
                for n in range(first, end):
                    j, kt = BLOCKS[n]
                    c = col + 128 * (n - first)
                    last = nc.tensor.transpose(ps[:, bank, c:c + 128],
                                               scores[:, a, S_OFF[j] + 128 * kt:S_OFF[j] + 128 * kt + 128], ident)
                last.then_inc(pt_done, 1)

            def score_products(a, par):
                hrow = slice(64 * a, 64 * a + 64)
                for j in Q_ORDER:
                    n = 128 * (j + 1)
                    qs = slice(128 * j, 128 * j + 128)
                    flat = ps[:, BANK_S:BANK_S + 3, :].rearrange("p b n -> p (b n)")
                    o = flat[:, S_OFF[j]:S_OFF[j] + n]
                    mm(o, q_stack[:, par, a, qs], k_stack[:, par, a, 0:n], start=True, stop=False)
                    last = mm(o, q_stack[hrow, par, a, qs], k_low[hrow, par, 0:n], start=False, stop=True)
                    if j != 2:
                        last.then_inc(s_done, 1)

            def pv_products(head):
                for n, (j, kt) in enumerate(BLOCKS):
                    mm(ps_o[:, j, :], pt[:, 0, n, :], v_split[:, kt, head, :], start=(kt == 0), stop=False)
                    last = mm(ps_o[:, j, 0:HD], pt[:, 1, n, :], v_split[:, kt, head, 0:HD], start=False,
                              stop=(kt == j))
                last.then_inc(pv_done, 1)

            pe.wait_ge(const_in, 32)
            for t in range(ST):
                pe.wait_ge(xn_done, t + 1)
                for hh in range(2):
                    n = 2 * t + hh
                    x_transposes(t, hh, n - 2, FIRST_XT[n % 3])
            pe.wait_ge(xt_low, 8)
            for c in range(CHUNKS):
                pe.wait_ge(w_low_done, CHUNKS * W_V + c + 1)
                v_product(0, 0, 0, range(KC * c, KC * (c + 1)), FIRST_V[0])
            v_product(1, 0, 0, range(KT), FIRST_V[1])
            pe.wait_ge(v_low, 1)
            v_product(2, 0, 0, range(KT), FIRST_V[2])
            for which, w in ((0, W_Q), (1, W_K)):
                if which == 0:
                    pe.wait_ge(v_low, 3)
                for c in range(CHUNKS):
                    pe.wait_ge(w_low_done, CHUNKS * w + c + 1)
                    qk_product(which, 0, 0, range(KC * c, KC * (c + 1)))
            v_product(3, 0, 0, range(KT), FIRST_V[3])

            def head_slot(b, kind, p, a):
                first, last_b = kind == 0, kind == B - 1
                bp = kind % 2
                g = 16 * b + 2 * p + a
                pr = 8 * b + p
                prev = not (first and p == 0 and a == 0)
                has_qk = not (last_b and p == PAIRS - 1)
                has_v = not (last_b and p >= 4)
                has_xt = not last_b and p < 4
                if a == 0:
                    need(pe, qk_low, 2 * pr + 2)
                    need(pe, qk_high, 2 * pr + 2)
                need(pe, masked, 4 * g)
                if prev:
                    need(pe, pt_low, 3 * g - 3)
                score_products(a, p % 2)
                if prev:
                    need(pe, exp_done, 4 * g)
                    pt_group(0, 1 - a)
                    pt_group(1, 1 - a)

                def late_transposes():
                    if prev:
                        need(pe, masked, 4 * g + 4)
                        pt_group(2, 1 - a)

                def pv():
                    if prev:
                        head = (2 * p + a - 1) % HEADS
                        need(pe, pt_high, 3 * g)
                        need(pe, pt_low, 3 * g)
                        if 0 < 2 * p + a:
                            need(pe, v_low, 8 * b + (4 if head < 8 else 8))
                        need(pe, o_added, g - 1)
                        pv_products(head)

                n_pair, n_par = (p + 1) % PAIRS, (p + 1) % 2
                n_bp = bp if p < PAIRS - 1 else 1 - bp
                v_bp = bp if p < 4 else 1 - bp
                if a == 0:
                    if has_qk:
                        need(pe, v_low, 4 + pr if not (last_b and p > 4) else 8 * B)
                        need(pe, qk_drained, 2 * pr + 2)
                        if p == PAIRS - 1:
                            need(pe, xt_low, 8 * b + 16)
                        qk_product(0, n_pair, n_bp, [0, 1, 2])
                    late_transposes()
                    if has_qk:
                        qk_product(0, n_pair, n_bp, [3, 4, 5, 6, 7])
                    pv()
                    if has_qk:
                        need(pe, xt_low, 8 * B if last_b else 8 * b + 8 + 2 * min(p, 4))
                        qk_product(1, n_pair, n_bp, range(KT))
                else:
                    if has_v:
                        need(pe, qk_drained, 2 * pr + 3)
                        if p == 4:
                            need(pe, xt_low, 8 * b + 16)
                        v_product(p % 4, 1 if p < 4 else 0, v_bp, [0, 1, 2])
                    late_transposes()
                    if has_xt:
                        need(pe, qk_drained, 2 * pr + 4)
                        need(pe, xn_done, 4 * b + 4 + p + 1)
                        x_transposes(p, 0, 8 * b + 8 + 2 * p)
                    if has_v:
                        v_product(p % 4, 1 if p < 4 else 0, v_bp, range(3, KT))
                    pv()
                    if has_xt:
                        x_transposes(p, 1, 8 * b + 8 + 2 * p + 1)

            def batch(b, kind):
                for p in range(PAIRS):
                    for a in range(2):
                        head_slot(b, kind, p, a)

            over_batches(pe, batch)
            g = HEADS * B
            pe.wait_ge(exp_done, 4 * g)
            pe.wait_ge(pt_low, 3 * g - 3)
            pt_group(0, 1)
            pt_group(1, 1)
            pt_group(2, 1)
            pe.wait_ge(pt_high, 3 * g)
            pe.wait_ge(pt_low, 3 * g)
            pe.wait_ge(o_added, g - 1)
            pv_products(HEADS - 1)

            def tile_transposes(src, done):
                for hh in range(2):
                    for k in range(4):
                        last = nc.tensor.transpose(ps[:, BANK_TR + hh, 128 * k:128 * k + 128],
                                                   src[:, 512 * hh + 128 * k:512 * hh + 128 * k + 128], ident)
                    last.then_inc(done, 1)

            def product(act_t, w, bank, last_one):
                for k in range(KT):
                    for hl, wl in ((0, 0), (0, 1), (1, 0)):
                        for c in range(2):
                            final = last_one and k == KT - 1 and hl == 1
                            last = mm(ps[:, bank + c, :], act_t[:, k, hl, :], w[:, k, wl, 512 * c:512 * c + 512],
                                      start=(k == 0 and hl == 0 and wl == 0), stop=final)
                return last

            def step(i, kind, i2):
                a = kind % 2

                def xn2_transposes():
                    need(pe, xn2_done, i)
                    if kind < TILES:
                        need(pe, ot_low, 2 * i + 2)
                    tile_transposes(xn2, x2t_done)

                if 2 <= kind <= TILES:
                    xn2_transposes()
                if kind < TILES:
                    if kind == 0:
                        pe.wait_ge(o_tile_in[0], 16)
                        pe.wait_ge(pt_low, 3 * g)
                        tile_transposes(o_in[:, 0], ot_done)
                        pe.wait_ge(w_low_done, CHUNKS * W_O + CHUNKS)
                    need(pe, ot_low, 2 * i + 2)
                    need(pe, ot_high, 2 * i + 2)
                    need(pe, u1_done, i)
                    product(o_t, region[2], BANK_AO, True).then_inc(ao_done, 1)
                if kind == 1:
                    xn2_transposes()
                if 1 <= kind <= TILES:
                    need(pe, x2t_low, 2 * i)
                    need(pe, x2t_high, 2 * i)
                    need(pe, lora_ready, 2)
                    need(pe, lt_scaled, i - 1)
                    for k in range(KT):
                        for ah, xh in ((0, 0), (0, 1), (1, 0)):
                            last = mm(ps[0:LR, BANK_T, 0:128], a_split[:, k, ah, :], xn2_t[:, k, xh, :],
                                      start=(k == 0 and ah == 0 and xh == 0), stop=(k == KT - 1 and ah == 1))
                    last.then_inc(lt_done, 1)
                if kind <= TILES - 2:
                    na = 1 - a
                    need(pe, o_tile_in[na], 16 * (i2 + 1 + a))
                    need(pe, x2t_low, 2 * i)
                    tile_transposes(o_in[:, na], ot_done)
                if 1 <= kind <= TILES:
                    if kind == 1:
                        pe.wait_ge(w_low_done, CHUNKS * W_F + CHUNKS)
                    need(pe, u2_done, i - 1)
                    product(xn2_t, region[0], BANK_FF, False)
                    need(pe, lt_low, i)
                    for c in range(2):
                        cols = slice(512 * c, 512 * c + 512)
                        mm(ps[:, BANK_FF + c, :], t_stack, b_split[:, 0, cols], start=False, stop=False)
                        last = mm(ps[:, BANK_FF + c, :], t_stack, b_split[:, 1, cols], start=False, stop=True)
                    last.then_inc(ff_done, 1)

            over_tiles(pe, step)

        @block.vector
        def _(dve):
            v = nc.vector
            steps = [0]

            def chained(ins):
                steps[0] += 1
                ins.then_inc(dve_step, 1)
                dve.wait_ge(dve_step, steps[0])

            def part_max(w, c):
                dve.wait_ge(raw_in[w][c], 16)
                v.tensor_reduce(w_part[:, w, c:c + 1], w_raw[w][:, KC * c:KC * (c + 1), :], AX.XY, ALU.max,
                                apply_absolute_value=True).then_inc(part_max_done, 1)

            def join_max(w):
                if w in (W_Q, W_K):
                    dve.wait_ge(squares_done, CHUNKS * w)
                else:
                    dve.wait_ge(part_max_done, CHUNKS * {W_V: 1, W_O: 2, W_F: 3}[w])
                v.tensor_reduce(w_pmax[:, w:w + 1], w_part[:, w, :], AX.X, ALU.max).then_inc(pmax_done, 1)

            def exponents(first, n):
                cols = slice(first, first + n)
                chained(v.tensor_scalar(expo_i[:, cols], w_max[:, cols].bitcast(I32), 23, None,
                                        ALU.logical_shift_right))
                chained(v.tensor_scalar(expo[:, cols], expo_i[:, cols], 30.0, None, ALU.max))

            def power(col, src, sign, plus):
                chained(v.tensor_scalar(field[:, 0:1], src, float(sign), float(plus), ALU.mult, ALU.add))
                chained(v.tensor_scalar(field_i[:, 0:1], field[:, 0:1], 1.0, 254.0, ALU.max, ALU.min))
                chained(v.tensor_scalar(pow2[:, col:col + 1].bitcast(I32), field_i[:, 0:1], 23, None,
                                        ALU.logical_shift_left))

            def weight_scale(w):
                dve.wait_ge(max_done, w + 1)
                if w in (W_Q, W_K):
                    chained(v.tensor_scalar(expo_i[:, w:w + 1], w_max[:, w:w + 1].bitcast(I32), 23, None,
                                            ALU.logical_shift_right))
                    chained(v.tensor_scalar(expo_i[:, w:w + 1], expo_i[:, w:w + 1], 127.0, None, ALU.add))
                    chained(v.tensor_scalar(expo_i[:, w:w + 1], expo_i[:, w:w + 1], 1, None,
                                            ALU.logical_shift_right))
                    chained(v.tensor_copy(expo[:, w:w + 1], expo_i[:, w:w + 1]))
                else:
                    exponents(w, 1)
                power(w, expo[:, w:w + 1], -1, 268)
                v.tensor_copy(pow2[:, 15:16], pow2[:, w:w + 1]).then_inc(scale_done, 1)

            def split_low(w, c):
                dve.wait_ge(w_high_done, CHUNKS * w + c + 1)
                ks = slice(KC * c, KC * (c + 1))
                v.scalar_tensor_tensor(w_dst[w][:, ks, 1, :], w_raw[w][:, ks, :], pow2[:, w:w + 1],
                                       w_dst[w][:, ks, 0, :], ALU.mult, ALU.subtract).then_inc(w_low_done, 1)

            def ln_stats(t, n):
                for c in range(2):
                    v.bn_stats(bn[:, t, c, :], x_ring[:, t, 512 * c:512 * c + 512]).then_inc(bn_done, 1)
                need(dve, bn_done, 2 * n + 2)
                v.nop(nofuse=True)
                v.bn_aggr(mean_var[:, t, :], bn[:, t, :, :].rearrange("p a b -> p (a b)")).then_inc(meanvar_done, 1)
                need(dve, meanvar_done, n + 1)
                v.tensor_scalar(var_s[:, t:t + 1], mean_var[:, t, 1:2], EPS, XS2, ALU.add,
                                ALU.mult).then_inc(var_done, 1)

            def ln_apply(t, n):
                need(dve, rstd_done, n + 1)
                v.tensor_scalar(x_ring[:, t, :], x_ring[:, t, :], mean_var[:, t, 0:1], rstd[:, t:t + 1],
                                ALU.subtract, ALU.mult).then_inc(xn_done, 1)

            def xt_evac(t, hh, par, n, bank=BANK_K):
                need(dve, xt_high, n + 1)
                dst = xnt[par][:, 4 * hh:4 * hh + 4, :, 128 * t:128 * t + 128]
                v.tensor_tensor(dst[:, :, 1, :], ps[:, bank, :].rearrange("p (k t) -> p k t", k=4),
                                dst[:, :, 0, :], ALU.subtract).then_inc(xt_low, 1)

            def v_evac(t, h8, n, bank=BANK_Q):
                need(dve, v_high, n + 1)
                dst = v_split[:, t, 8 * h8:8 * h8 + 8, :]
                v.scalar_tensor_tensor(dst[:, :, HD:2 * HD], ps[:, bank, :].rearrange("p (h c) -> p h c", h=8),
                                       V_DOWN, dst[:, :, 0:HD], ALU.mult, ALU.subtract).then_inc(v_low, 1)

            def qk_drain(which, n):
                bank = (BANK_Q, BANK_K)[which]
                need(dve, qk_done, n + 1)
                need(dve, qk_high, n)
                need(dve, qk_low, n)
                v.tensor_tensor(rotated[:, :], ps[:, bank, :], cos_t, ALU.mult)
                v.stream_shuffle(swapped[:, :], ps[:, bank, :], [r ^ 1 for r in range(32)]).then_inc(qk_drained, 1)

            def qk_low_parts(which, par, n):
                need(dve, rot_done, n + 1)
                if which == 1:
                    for a in range(2):
                        rows = slice(64 * a, 64 * a + 64)
                        last = v.tensor_copy(k_stack[rows, par, a, :], rotated[rows, :])
                    last.then_inc(qk_high, 1)
                need(dve, qk_high, n + 1)
                if which == 0:
                    v.tensor_tensor(q_stack[64:128, par, 0, :], rotated[0:64, :], q_stack[0:64, par, 0, :],
                                    ALU.subtract)
                    v.tensor_tensor(q_stack[0:64, par, 1, :], rotated[64:128, :], q_stack[64:128, par, 1, :],
                                    ALU.subtract).then_inc(qk_low, 1)
                else:
                    for a in range(2):
                        rows, others = slice(64 * a, 64 * a + 64), slice(64 - 64 * a, 128 - 64 * a)
                        v.tensor_tensor(k_low[rows, par, :], rotated[rows, :], k_stack[rows, par, a, :],
                                        ALU.subtract)
                        last = v.tensor_copy(k_stack[others, par, a, :], k_stack[rows, par, a, :])
                    last.then_inc(qk_low, 1)

            def pt_evac(grp, h):
                first, end = PT_GROUPS[grp]
                bank, col = PT_PLACE[grp]
                need(dve, pt_high, 3 * h + grp + 1)
                src = ps[:, bank, col:col + 128 * (end - first)].rearrange("p (n q) -> p n q", q=PART)
                v.tensor_tensor(pt[:, 1, first:end, :], src, pt[:, 0, first:end, :], ALU.subtract).then_inc(pt_low, 1)

            dve.wait_ge(const_in, 32)
            for t in range(ST):
                dve.wait_ge(x_in[t], 16)
                ln_stats(t, t)
            for t in range(ST):
                ln_apply(t, t)
            for n in range(2 * ST):
                xt_evac(n // 2, n % 2, 0, n, FIRST_XT[n % 3])
                if n % 2 == 1:
                    part_max(W_V, n // 2)
            join_max(W_V)
            weight_scale(W_V)
            for c in range(CHUNKS):
                split_low(W_V, c)
            v_evac(0, 0, 0, FIRST_V[0])
            join_max(W_Q)
            weight_scale(W_Q)
            split_low(W_Q, 0)
            v_evac(1, 0, 1, FIRST_V[1])
            for c in range(1, CHUNKS):
                split_low(W_Q, c)
            v_evac(2, 0, 2, FIRST_V[2])
            join_max(W_K)
            weight_scale(W_K)
            chained(v.tensor_tensor(expo[:, 8:9], expo[:, W_Q:W_Q + 1], expo[:, W_K:W_K + 1], ALU.add))
            power(S_SM, expo[:, 8:9], 1, -136)
            chained(v.tensor_scalar(pow2[:, S_NEG:S_NEG + 1], pow2[:, S_SM:S_SM + 1], -1.0, None, ALU.mult))
            split_low(W_K, 0)
            split_low(W_K, 1)
            qk_drain(0, 0)
            split_low(W_K, 2)
            split_low(W_K, 3)
            qk_low_parts(0, 0, 0)
            qk_drain(1, 1)
            qk_low_parts(1, 0, 1)
            v_evac(3, 0, 3, FIRST_V[3])
            chained(v.tensor_copy(starts_f[:, :], starts_i[:, :]))
            for n in range(NSEG):
                chained(v.tensor_scalar(le[:, n, :], con[0:LR, C_TB:C_TB + TILES], starts_f[:, n:n + 1], None,
                                        ALU.is_ge))
            c0, c1, c2, c3 = (le[:, n, :] for n in range(NSEG))
            chained(v.tensor_scalar(adapter[:, :], c0, -1.0, 2.0, ALU.mult, ALU.add))
            chained(v.tensor_tensor(adapter[:, :], adapter[:, :], c1, ALU.mult))
            chained(v.tensor_tensor(c0, adapter[:, :], c0, ALU.add))
            chained(v.scalar_tensor_tensor(c3, c3, 3.0, c0, ALU.add, ALU.subtract))
            chained(v.tensor_tensor(c3, c3, c2, ALU.mult))
            chained(v.tensor_tensor(c3, c3, c0, ALU.add))
            chained(v.tensor_scalar(adapter[:, :], c3, con[0:LR, C_CODE:C_CODE + 1], None, ALU.is_equal))

            def clear_lora():
                dve.wait_ge(qk_done, 2 * PAIRS * B)
                chained(v.memset(b_raw, 0.0))
                chained(v.memset(b_split[:, 1, :], 0.0))
                chained(v.memset(t_stack, 0.0))
                chained(v.memset(t_stack[32:64, :], ONE))
                v.tensor_scalar(pow2[:, S_NOTBIAS:S_NOTBIAS + 1], con[:, C_BIASROW:C_BIASROW + 1], -1.0, 1.0,
                                ALU.mult, ALU.add).then_inc(lora_ready, 1)

            def lora_max():
                dve.wait_ge(lora_ready, 1)
                dve.wait_ge(lora_in, 64)
                chained(v.tensor_reduce(w_pmax[:, 5:6], a_raw, AX.XY, ALU.max, apply_absolute_value=True))
                chained(v.tensor_reduce(field[:, 1:2], b_raw, AX.X, ALU.max, apply_absolute_value=True))
                chained(v.tensor_tensor(w_pmax[:, 6:7], field[:, 1:2], pow2[:, S_NOTBIAS:S_NOTBIAS + 1], ALU.mult))
                v.tensor_tensor(w_pmax[:, 7:8], field[:, 1:2], con[:, C_BIASROW:C_BIASROW + 1],
                                ALU.mult).then_inc(pmax_done, 1)

            def head_slot(b, kind, p, a):
                first, last_b = kind == 0, kind == B - 1
                g = 16 * b + 2 * p + a
                pr = 8 * b + p
                prev = not (first and p == 0 and a == 0)
                has_qk = not (last_b and p == PAIRS - 1)
                bp = kind % 2
                if a == 0:
                    if not (first and p == 0) and not (last_b and p > 4):
                        q = (p - 1) % 8
                        v_evac(q % 4, 1 if q < 4 else 0, 3 + pr)
                    if not last_b and 1 <= p <= 4:
                        xt_evac(p - 1, 1, 1 - bp, 8 * b + 8 + 2 * p - 1)
                if a == 1 and has_qk:
                    qk_drain(1, 2 * pr + 3)

                for n, j in enumerate(Q_ORDER):
                    width = 128 * (j + 1)
                    flat = ps[:, BANK_S:BANK_S + 3, :].rearrange("p b n -> p (b n)")
                    cols = slice(S_OFF[j], S_OFF[j] + width)
                    if j != 0:
                        need(dve, s_done, 3 * g + {3: 1, 2: 2, 1: 3}[j])
                    if n == 0:
                        need(dve, pt_done, 3 * g - 3)
                    v.nop(nofuse=True)
                    v.tensor_tensor_reduce(out=scores[:, a, cols], in0=flat[:, cols], in1=causal[:, 512 - width:512],
                                           scale=1.0, scalar=LOWEST, op0=ALU.add, op1=ALU.max,
                                           accum_out=row_max[:, a, j:j + 1]).then_inc(masked, 1)
                need(dve, masked, 4 * g + 4)
                v.tensor_scalar(exp_bias[:, a, :], row_max[:, a, :], pow2[:, S_NEG:S_NEG + 1], P_LOG, ALU.mult,
                                ALU.add).then_inc(bias_done, 1)
                if prev:
                    pt_evac(0, g - 1)
                    pt_evac(1, g - 1)
                if a == 1 and has_qk:
                    qk_low_parts(1, (p + 1) % 2, 2 * pr + 3)
                if prev:
                    pt_evac(2, g - 1)
                if a == 1 and not last_b and p < 4:
                    xt_evac(p, 0, 1 - bp, 8 * b + 8 + 2 * p)
                if a == 0 and has_qk:
                    qk_drain(0, 2 * pr + 2)
                if last_b and p in (1, 2):
                    part_max(W_O, 2 * (p - 1) + a)
                if last_b and p >= 6:
                    part_max(W_F, 2 * (p - 6) + a)
                if last_b and p == 3:
                    if a == 0:
                        join_max(W_O)
                    else:
                        weight_scale(W_O)
                        chained(v.tensor_tensor(expo[:, 9:10], expo[:, W_V:W_V + 1], expo[:, W_O:W_O + 1], ALU.add))
                        power(S_KAPPA, expo[:, 9:10], 1, -145)
                if last_b and p in (4, 5):
                    split_low(W_O, 2 * (p - 4) + a)
                if not last_b and p < 4:
                    if a == 0:
                        need(dve, x_in[p], 16 * (b + 2))
                        ln_stats(p, 4 * b + 4 + p)
                if prev:
                    h = g - 1
                    need(dve, exp_done, 4 * h + 4)
                    need(dve, o_ready, h)
                    v.reciprocal(row_inv[:, 1 - a, :], row_sum[:, 1 - a, :]).then_inc(inv_done, 1)
                    need(dve, o_copied, h + 1)
                    v.tensor_tensor(o_sum_t[:, :, :], ps_o[:, :, 0:HD], o_low[:, :, :], ALU.add).then_inc(o_added, 1)
                if a == 0 and has_qk:
                    qk_low_parts(0, (p + 1) % 2, 2 * pr + 2)
                if a == 0 and not last_b and p < 4:
                    ln_apply(p, 4 * b + 4 + p)
                if last_b and (p, a) == (PAIRS - 2, 1):
                    clear_lora()
                if last_b and p == PAIRS - 1:
                    if a == 0:
                        lora_max()
                    else:
                        join_max(W_F)

            def batch(b, kind):
                for p in range(PAIRS):
                    for a in range(2):
                        head_slot(b, kind, p, a)

            over_batches(dve, batch)
            h = HEADS * B - 1
            for grp in range(3):
                pt_evac(grp, h)
            dve.wait_ge(exp_done, 4 * h + 4)
            dve.wait_ge(o_ready, h)
            v.reciprocal(row_inv[:, 1, :], row_sum[:, 1, :]).then_inc(inv_done, 1)
            dve.wait_ge(o_copied, h + 1)
            v.tensor_tensor(o_sum_t[:, :, :], ps_o[:, :, 0:HD], o_low[:, :, :], ALU.add).then_inc(o_added, 1)

            def low_of(grp, bank, dst, high_done, n, done):
                need(dve, high_done, n)
                ks = slice(4 * grp, 4 * grp + 4)
                v.tensor_tensor(dst[:, ks, 1, :], ps[:, bank, :].rearrange("p (k t) -> p k t", k=4),
                                dst[:, ks, 0, :], ALU.subtract).then_inc(done, 1)

            def stats(src, st, mv, bn_sem, mv_sem, n):
                for c in range(2):
                    v.bn_stats(st[:, c, :], src[c]).then_inc(bn_sem, 1)
                need(dve, bn_sem, 2 * n + 2)
                v.nop(nofuse=True)
                v.bn_aggr(mv[:, :], st[:, :, :].rearrange("p a b -> p (a b)")).then_inc(mv_sem, 1)
                need(dve, mv_sem, n + 1)

            def true_variance(sm, mv, unscale, done, n):
                v.tensor_scalar(sm[:, 3:4], mv[:, 1:2], unscale, unscale, ALU.mult, ALU.mult).then_inc(done, 1)
                need(dve, done, 2 * n + 1)
                v.tensor_scalar(sm[:, 0:1], sm[:, 3:4], EPS, None, ALU.add).then_inc(done, 1)

            def scale_and_shift(sm, mv, unscale, powered, done, n):
                need(dve, powered, n + 1)
                v.tensor_scalar(sm[:, 1:2], sm[:, 0:1], unscale, None, ALU.mult).then_inc(done, 1)
                need(dve, done, 2 * n + 1)
                v.tensor_scalar(sm[:, 2:3], mv[:, 0:1], sm[:, 1:2], -1.0, ALU.mult, ALU.mult).then_inc(done, 1)

            kappa = pow2[:, S_KAPPA:S_KAPPA + 1]
            kf = pow2[:, S_KF:S_KF + 1]
            for grp in range(2):
                low_of(grp, BANK_TR + grp, o_t, ot_high, grp + 1, ot_low)
            dve.wait_ge(max_done, W_F + 1)
            exponents(4, 4)
            chained(v.tensor_tensor(expo[:, 10:11], expo[:, 5:6], expo[:, 6:7], ALU.add))
            chained(v.tensor_scalar(expo[:, 10:11], expo[:, 10:11], -121.0, None, ALU.add))
            chained(v.tensor_scalar(expo[:, 11:12], expo[:, 7:8], -4.0, None, ALU.add))
            chained(v.tensor_tensor(expo[:, 11:12], expo[:, 11:12], expo[:, 10:11], ALU.max))
            chained(v.tensor_tensor(expo[:, 11:12], expo[:, 11:12], expo[:, 4:5], ALU.max))
            power(W_F, expo[:, 11:12], -1, 268)
            v.tensor_copy(pow2[:, 15:16], pow2[:, W_F:W_F + 1]).then_inc(scale_done, 1)
            power(S_A, expo[:, 5:6], -1, 268)
            chained(v.tensor_tensor(expo[:, 10:11], expo[:, 5:6], expo[:, 11:12], ALU.subtract))
            power(S_B, expo[:, 10:11], 1, 147)
            power(S_BIAS, expo[:, 11:12], -1, 264)
            power(S_KF, expo[:, 11:12], 1, -24)
            chained(v.tensor_tensor(pow2[:, S_B:S_B + 1], pow2[:, S_B:S_B + 1], pow2[:, S_NOTBIAS:S_NOTBIAS + 1],
                                    ALU.mult))
            chained(v.tensor_tensor(pow2[:, S_BIAS:S_BIAS + 1], pow2[:, S_BIAS:S_BIAS + 1],
                                    con[:, C_BIASROW:C_BIASROW + 1], ALU.mult))
            chained(v.tensor_tensor(pow2[:, S_ROWS:S_ROWS + 1], pow2[:, S_B:S_B + 1], pow2[:, S_BIAS:S_BIAS + 1],
                                    ALU.add))
            chained(v.tensor_scalar(a_split[:, :, 0, :], a_raw, pow2[:, S_A:S_A + 1], None, ALU.mult))
            chained(v.scalar_tensor_tensor(a_split[:, :, 1, :], a_raw, pow2[:, S_A:S_A + 1], a_split[:, :, 0, :],
                                           ALU.mult, ALU.subtract))
            chained(v.tensor_scalar(b_split[:, 0, :], b_raw, pow2[:, S_ROWS:S_ROWS + 1], None, ALU.mult))
            v.scalar_tensor_tensor(b_split[0:LOW_ROW, 1, :], b_raw[0:LOW_ROW, :], pow2[0:LOW_ROW, S_ROWS:S_ROWS + 1],
                                   b_split[0:LOW_ROW, 0, :], ALU.mult, ALU.subtract).then_inc(lora_ready, 1)
            split_low(W_F, 0)
            split_low(W_F, 1)

            ps_ff = [ps[:, BANK_FF + c, :] for c in range(2)]
            ps_ao = [ps[:, BANK_AO + c, :] for c in range(2)]

            def step(i, kind, i2):
                a = kind % 2
                if kind >= 2:
                    need(dve, ff_done, i - 1)
                    stats(ps_ff, st2, mv2, bn2_done, mv2_done, i - 2)
                    true_variance(sm2, mv2, kf, var2_done, i - 2)
                if 1 <= kind <= TILES:
                    for grp in range(2):
                        low_of(grp, BANK_TR + grp, xn2_t, x2t_high, 2 * i - 1 + grp, x2t_low)
                if kind >= 2:
                    scale_and_shift(sm2, mv2, kf, pow2_done, rm2_done, i - 2)
                    need(dve, u2_done, i - 1)
                    need(dve, y_stored[a], 16 * (i2 - 1))
                    v.tensor_tensor(y_out[:, a], x2[:, a], u2, ALU.add).then_inc(y_done, 1)
                if kind < TILES:
                    need(dve, ao_done, i + 1)
                    stats(ps_ao, st1, mv1, bn1_done, mv1_done, i)
                    true_variance(sm1, mv1, kappa, var1_done, i)
                if 1 <= kind <= TILES:
                    need(dve, lt_done, i)
                    v.tensor_scalar(t_f, ps[0:LR, BANK_T, 0:128], T_DOWN, adapter[:, bass.ds(i - 1, 1)], ALU.mult,
                                    ALU.mult).then_inc(lt_scaled, 1)
                    need(dve, lt_scaled, i)
                    v.tensor_copy(t_stack[0:LR, :], t_f).then_inc(lt_high, 1)
                    need(dve, lt_high, i)
                    v.tensor_tensor(t_stack[LOW_ROW:LOW_ROW + LR, :], t_f, t_stack[0:LR, :],
                                    ALU.subtract).then_inc(lt_low, 1)
                if kind < TILES:
                    scale_and_shift(sm1, mv1, kappa, pow1_done, rm1_done, i)
                if kind <= TILES - 2:
                    for grp in range(2):
                        low_of(grp, BANK_TR + grp, o_t, ot_high, 2 * i + 3 + grp, ot_low)
                if kind < TILES:
                    need(dve, u1_done, i + 1)
                    need(dve, x_tile_in[a], 16 * (i2 + 1))
                    v.tensor_tensor(x2[:, a], x2[:, a], u1, ALU.add).then_inc(x2_done, 1)
                    need(dve, x2_done, i + 1)
                    stats([x2[:, a, 512 * c:512 * c + 512] for c in range(2)], stx, mvx, bnx_done, mvx_done, i)
                    v.tensor_scalar(smx[:, 0:1], mvx[:, 1:2], EPS, XS2, ALU.add, ALU.mult).then_inc(varx_done, 1)
                    need(dve, powx_done, i + 1)
                    v.tensor_scalar(xn2, x2[:, a], mvx[:, 0:1], smx[:, 1:2], ALU.subtract,
                                    ALU.mult).then_inc(xn2_done, 1)
                if kind == 0:
                    split_low(W_F, 2)
                    split_low(W_F, 3)

            over_tiles(dve, step)

        @block.scalar
        def _(act):
            s = nc.scalar

            def split_high(w, c):
                act.wait_ge(scale_done, w + 1)
                act.wait_ge(raw_in[w][c], 16)
                ks = slice(KC * c, KC * (c + 1))
                s.activation(w_dst[w][:, ks, 0, :], w_raw[w][:, ks, :], ACT.Copy,
                             scale=pow2[:, w:w + 1]).then_inc(w_high_done, 1)

            def xt_evac(t, hh, par, n, bank=BANK_K):
                need(act, xt_done, n + 1)
                dst = xnt[par][:, 4 * hh:4 * hh + 4, 0, 128 * t:128 * t + 128]
                s.activation(dst, ps[:, bank, :].rearrange("p (k t) -> p k t", k=4),
                             ACT.Copy).then_inc(xt_high, 1)

            def v_evac(t, h8, n, bank=BANK_Q):
                need(act, v_done, n + 1)
                s.activation(v_split[:, t, 8 * h8:8 * h8 + 8, 0:HD],
                             ps[:, bank, :].rearrange("p (h c) -> p h c", h=8), ACT.Copy,
                             scale=V_DOWN).then_inc(v_high, 1)

            def q_high_parts(par, n):
                need(act, rot_done, n + 1)
                for a in range(2):
                    rows = slice(64 * a, 64 * a + 64)
                    last = s.activation(q_stack[rows, par, a, :], rotated[rows, :], ACT.Copy)
                last.then_inc(qk_high, 1)

            def pt_evac(grp, h):
                first, end = PT_GROUPS[grp]
                bank, col = PT_PLACE[grp]
                need(act, pt_done, 3 * h + grp + 1)
                src = ps[:, bank, col:col + 128 * (end - first)].rearrange("p (n q) -> p n q", q=PART)
                s.activation(pt[:, 0, first:end, :], src, ACT.Copy).then_inc(pt_high, 1)

            def o_copy(h):
                need(act, pv_done, h + 1)
                need(act, o_added, h)
                s.activation(o_low[:, :, :], ps_o[:, :, HD:2 * HD], ACT.Copy).then_inc(o_copied, 1)

            def squares(w, c):
                act.wait_ge(raw_in[w][c], 16)
                if (w, c) != (W_Q, 0):
                    act.wait_ge(squares_done, CHUNKS * (w - W_Q) + c)
                s.activation(ps[:, BANK_SQUARES:BANK_SQUARES + 4, :].rearrange("p b n -> p (b n)"),
                             w_raw[w][:, KC * c:KC * (c + 1), :].rearrange("p k n -> p (k n)"), ACT.Square,
                             accum_out=w_part[:, w, c:c + 1]).then_inc(squares_done, 1)

            for n in range(2 * ST):
                xt_evac(n // 2, n % 2, 0, n, FIRST_XT[n % 3])
            for c in range(CHUNKS):
                split_high(W_V, c)
            squares(W_Q, 0)
            squares(W_Q, 1)
            v_evac(0, 0, 0, FIRST_V[0])
            squares(W_Q, 2)
            squares(W_Q, 3)
            split_high(W_Q, 0)
            v_evac(1, 0, 1, FIRST_V[1])
            for c in range(1, CHUNKS):
                split_high(W_Q, c)
            v_evac(2, 0, 2, FIRST_V[2])
            for c in range(CHUNKS):
                squares(W_K, c)
            act.wait_ge(w_low_done, CHUNKS * (W_Q + 1))
            for c in range(CHUNKS):
                split_high(W_K, c)
            q_high_parts(0, 0)
            v_evac(3, 0, 3, FIRST_V[3])

            def head_slot(b, kind, p, a):
                first, last_b = kind == 0, kind == B - 1
                g = 16 * b + 2 * p + a
                pr = 8 * b + p
                prev = not (first and p == 0 and a == 0)
                has_qk = not (last_b and p == PAIRS - 1)
                bp = kind % 2
                if a == 0:
                    if not (first and p == 0) and not (last_b and p > 4):
                        q = (p - 1) % 8
                        v_evac(q % 4, 1 if q < 4 else 0, 3 + pr)
                    if not last_b and 1 <= p <= 4:
                        xt_evac(p - 1, 1, 1 - bp, 8 * b + 8 + 2 * p - 1)
                if prev:
                    pt_evac(0, g - 1)
                    pt_evac(1, g - 1)
                need(act, bias_done, g + 1)
                for j in Q_ORDER:
                    cols = slice(S_OFF[j], S_OFF[j] + 128 * (j + 1))
                    s.activation(scores[:, a, cols], scores[:, a, cols], ACT.Exp, bias=exp_bias[:, a, j:j + 1],
                                 scale=pow2[:, S_SM:S_SM + 1],
                                 accum_out=row_sum[:, a, j:j + 1]).then_inc(exp_done, 1)
                    if prev and j == 2:
                        pt_evac(2, g - 1)
                if last_b and p in (4, 5):
                    if p == 4 and a == 0:
                        act.wait_ge(v_done, 8 * B)
                    split_high(W_O, 2 * (p - 4) + a)
                if prev and a == 0:
                    o_copy(g - 1)
                if a == 1 and not last_b and p < 4:
                    xt_evac(p, 0, 1 - bp, 8 * b + 8 + 2 * p)
                if a == 0 and has_qk:
                    q_high_parts((p + 1) % 2, 2 * pr + 2)
                if a == 1:
                    o_copy(g - 1)

            def batch(b, kind):
                for p in range(PAIRS):
                    for a in range(2):
                        head_slot(b, kind, p, a)

            over_batches(act, batch)
            for grp in range(3):
                pt_evac(grp, HEADS * B - 1)
            o_copy(HEADS * B - 1)

            def high_of(grp, bank, dst, made, n, done):
                need(act, made, n)
                s.activation(dst[:, 4 * grp:4 * grp + 4, 0, :], ps[:, bank, :].rearrange("p (k t) -> p k t", k=4),
                             ACT.Copy).then_inc(done, 1)

            def normalise(u, bank, sm, ready, n, done):
                need(act, ready, 2 * n + 2)
                s.activation(u.rearrange("p (c n) -> p c n", c=2), ps[:, bank:bank + 2, :], ACT.Identity,
                             bias=sm[:, 2:3], scale=sm[:, 1:2]).then_inc(done, 1)

            for grp in range(2):
                high_of(grp, BANK_TR + grp, o_t, ot_done, grp + 1, ot_high)
            split_high(W_F, 0)
            split_high(W_F, 1)

            def step(i, kind, i2):
                if 1 <= kind <= TILES:
                    for grp in range(2):
                        high_of(grp, BANK_TR + grp, xn2_t, x2t_done, 2 * i - 1 + grp, x2t_high)
                if kind >= 2:
                    need(act, y_done, i - 2)
                    normalise(u2, BANK_FF, sm2, rm2_done, i - 2, u2_done)
                if kind <= TILES - 2:
                    need(act, ao_done, i + 1)
                    for grp in range(2):
                        high_of(grp, BANK_TR + grp, o_t, ot_done, 2 * i + 3 + grp, ot_high)
                if kind < TILES:
                    need(act, x2_done, i)
                    normalise(u1, BANK_AO, sm1, rm1_done, i, u1_done)
                if kind == 0:
                    split_high(W_F, 2)
                    split_high(W_F, 3)

            over_tiles(act, step)

        @block.gpsimd
        def _(pool):
            gp = nc.gpsimd
            minus_half = con[:, C_HALF:C_HALF + 1]

            def weight_max(w, n):
                pool.wait_ge(pmax_done, w + 1 + (1 if w == W_F else 0))
                gp.partition_all_reduce(w_max[:, w:w + n], w_pmax[:, w:w + n], PART, ABSMAX).then_inc(max_done, 1)

            def ln_rstd(t, n):
                need(pool, var_done, n + 1)
                gp.tensor_tensor(rstd[:, t:t + 1], var_s[:, t:t + 1], minus_half, ALU.pow).then_inc(rstd_done, 1)

            def rotate(n):
                need(pool, qk_drained, n + 1)
                gp.tensor_tensor(swapped[:, :], swapped[:, :], sin_t, ALU.mult).then_inc(rot_mul, 1)
                need(pool, rot_mul, n + 1)
                gp.tensor_tensor(rotated[:, :], rotated[:, :], swapped[:, :], ALU.add).then_inc(rot_done, 1)

            def o_scale(h, a, p, stored):
                need(pool, o_added, h + 1)
                need(pool, inv_done, h + 1)
                if a == 0:
                    need(pool, o_stored[p % 2], stored)
                gp.tensor_tensor(o_pair[:, p % 2, :, 64 * a:64 * a + 64], o_sum_t[:, :, :],
                                 row_inv[:, a, :].unsqueeze(2).broadcast_to([PART, ST, HD]),
                                 ALU.mult).then_inc(o_ready, 1)

            pool.wait_ge(const_in, 32)
            for t in range(ST):
                ln_rstd(t, t)
            for w in (W_V, W_Q, W_K):
                weight_max(w, 1)
            rotate(0)
            rotate(1)

            def batch(b, kind):
                first, last_b = kind == 0, kind == B - 1
                for p in range(PAIRS):
                    for a in range(2):
                        g = 16 * b + 2 * p + a
                        pr = 8 * b + p
                        if last_b and p == 3 and a == 0:
                            weight_max(W_O, 1)
                        if a == 1 and not (last_b and p == PAIRS - 1):
                            rotate(2 * pr + 3)
                        if a == 0 and not (last_b and p == PAIRS - 1):
                            rotate(2 * pr + 2)
                        if not last_b and p < 4 and a == 0:
                            ln_rstd(p, 4 * b + 4 + p)
                        if not (first and p == 0 and a == 0):
                            if a == 1:
                                o_scale(g - 1, 0, p, 16 * (4 * b + p // 2))
                            else:
                                o_scale(g - 1, 1, p - 1, 0)

            over_batches(pool, batch)
            weight_max(W_F, 4)
            o_scale(HEADS * B - 1, 1, PAIRS - 1, 0)

            def power_half(sm, out_col, ready, n, done):
                need(pool, ready, n)
                gp.tensor_tensor(sm[:, out_col:out_col + 1], sm[:, 0:1], minus_half, ALU.pow).then_inc(done, 1)

            def step(i, kind, i2):
                if kind >= 2:
                    power_half(sm2, 0, var2_done, 2 * (i - 2) + 2, pow2_done)
                if kind < TILES:
                    power_half(sm1, 0, var1_done, 2 * i + 2, pow1_done)
                    power_half(smx, 1, varx_done, i + 1, powx_done)

            over_tiles(pool, step)


def _constants():
    import numpy as np

    c = np.zeros((PART, C_LEN), np.float32)
    c[:, C_ID:C_ID + 128] = np.eye(128, dtype=np.float32)
    r = np.arange(PART)
    c[:, C_MASK + 384:C_MASK + 512] = np.where(r[None, :] > r[:, None], np.float32(NEG), np.float32(0))
    inv_freq = np.float32(1) / (np.float32(10000) ** (np.arange(0, HD, 2, dtype=np.float32) / np.float32(HD)))
    angle = np.arange(S, dtype=np.float32)[None, :] * inv_freq[(r % HD) // 2][:, None]
    c[:, C_COS:C_COS + S] = np.cos(angle.astype(np.float64)).astype(np.float32) * np.float32(QK_DOWN)
    c[:, C_SIN:C_SIN + S] = np.sin(angle.astype(np.float64)).astype(np.float32) * np.float32(QK_DOWN)
    c[LR, C_BIASROW] = 1
    c[:, C_TB:C_TB + TILES] = np.arange(TILES) // ST
    c[:LR, C_CODE] = np.arange(LR) // RANK + 2
    c[:, C_HALF:C_HALF + 4] = -0.5
    return c


def kernel(**inputs):
    import numpy as _np
    import concourse.bacc as _bacc
    from concourse import mybir as _mybir
    from concourse.bass_utils import run_bass_kernel_spmd as _run

    a = {k: _np.asarray(v) for k, v in inputs.items()}
    lora_b = a["L0_ffn_lora_B"]
    arrays = {
        "x": a["L0_attn_hidden_states"],
        "wq": a["L0_attn_Wq"],
        "wk": a["L0_attn_Wk"],
        "wv": a["L0_attn_Wv"],
        "wo": a["L0_attn_Wo"],
        "wf": a["L0_ffn_weight"].T,
        "bias": a["L0_ffn_bias"].reshape(1, D),
        "lora_a": a["L0_ffn_lora_A"].reshape(LR, D).T,
        "lora_b": lora_b.transpose(0, 2, 1).reshape(LR, D),
        "starts": _np.broadcast_to(a["L0_ffn_lora_start_indices"].reshape(1, NSEG), (LR, NSEG)),
        "consts": _constants(),
    }
    arrays = {k: _np.ascontiguousarray(v) for k, v in arrays.items()}
    nc = _bacc.Bacc("TRN2", target_bir_lowering=False, num_devices=1)
    args = [nc.dram_tensor(k, v.shape, _mybir.dt.from_np(v.dtype), kind="ExternalInput").ap()
            for k, v in arrays.items()]
    out = nc.dram_tensor("out", (B, S, D), F32, kind="ExternalOutput").ap()
    sandwich_kernel(nc, *args, out)
    r = _run(nc, [arrays], core_ids=[0])
    return r.results[0]["out"]
```
